# Optimizing a Trainium2 kernel written in Bass

```python
import numpy as np
import jax
import jax.numpy as jnp

def _softmax(x, axis=-1):
    return jax.nn.softmax(x, axis=axis)

def _gelu(x):
    return jax.nn.gelu(x, approximate=True)

def _silu(x):
    return jax.nn.silu(x)

def _sigmoid(x):
    return jax.nn.sigmoid(x)

def _layernorm(x, axis=-1, eps=1e-05):
    m = jnp.mean(x, axis=axis, keepdims=True)
    v = jnp.var(x, axis=axis, keepdims=True)
    return (x - m) / jnp.sqrt(v + eps)

def _scatter_add(tgt, idx, src, axis=0):
    return tgt.at[idx].add(src)

def _segment_sum(src, seg, n):
    return jax.ops.segment_sum(src, seg, n)
kernel_name = 'mk_macaron_d1_jaxref_r8_3621d6'

def setup_inputs(seed: int=0):
    np.random.seed(seed)
    _w = jnp.asarray

    def _L0_attn_setup():
        import jax, jax.numpy as jnp
        import numpy as np
        B, N, DE, H, DH = (2, 128, 128, 16, 64)
        DK = H * DH
        MIN_EXP = -30.0
        EPS = 0.0001
        key = jax.random.key(seed)
        ks = jax.random.split(key, 8)

        def g(i, shape, sc=1.0):
            return jax.random.normal(ks[i], shape, jnp.float32) * sc
        freqs = 10000.0 ** (-np.arange(DH // 2, dtype=np.float64) / (DH // 2))
        omega = jnp.asarray(np.tile(freqs[None, :], (H, 1)), jnp.float32)
        return {'x': g(0, (B, N, DE)), 'Wq': g(1, (DE, 2 * DK), 1.0 / np.sqrt(DE)), 'Wk': g(2, (DE, 2 * DK), 1.0 / np.sqrt(DE)), 'Wv': g(3, (DE, 2 * DK), 1.0 / np.sqrt(DE)), 'Wo': g(4, (2 * DK, DE), 1.0 / np.sqrt(2 * DK)), 'omega': omega, 'mu_raw': g(5, (H,)) - 2.0, 'sigma_raw': g(6, (H,)), 'eta_raw': jnp.ones((H,), jnp.float32), 'gamma_raw': jnp.ones((H,), jnp.float32), 'tau': jnp.ones((H,), jnp.float32), 'nu_raw': jnp.ones((H,), jnp.float32) * 4.0}
    _L0_attn_in = _L0_attn_setup()

    def _L0_ffn_setup():
        import jax, jax.numpy as jnp
        import numpy as np
        B, S, D = (4, 256, 128)
        E, K = (8, 2)
        H = 176
        key = jax.random.key(seed)
        kx, kr, k1, k2, k3 = jax.random.split(key, 5)
        s = 0.02
        return {'x': jax.random.normal(kx, (B, S, D), dtype=jnp.float32), 'w_router': jax.random.normal(kr, (E, D), dtype=jnp.float32) * s, 'w1': jax.random.normal(k1, (E, D, H), dtype=jnp.float32) * s, 'w2': jax.random.normal(k2, (E, H, D), dtype=jnp.float32) * s, 'w3': jax.random.normal(k3, (E, D, H), dtype=jnp.float32) * s}
    _L0_ffn_in = _L0_ffn_setup()
    _d = {'L0_attn_x': _L0_attn_in['x'], 'L0_attn_Wq': _L0_attn_in['Wq'], 'L0_attn_Wk': _L0_attn_in['Wk'], 'L0_attn_Wv': _L0_attn_in['Wv'], 'L0_attn_Wo': _L0_attn_in['Wo'], 'L0_attn_omega': _L0_attn_in['omega'], 'L0_attn_mu_raw': _L0_attn_in['mu_raw'], 'L0_attn_sigma_raw': _L0_attn_in['sigma_raw'], 'L0_attn_eta_raw': _L0_attn_in['eta_raw'], 'L0_attn_gamma_raw': _L0_attn_in['gamma_raw'], 'L0_attn_tau': _L0_attn_in['tau'], 'L0_attn_nu_raw': _L0_attn_in['nu_raw'], 'L0_ffn_w_router': _L0_ffn_in['w_router'], 'L0_ffn_w1': _L0_ffn_in['w1'], 'L0_ffn_w2': _L0_ffn_in['w2'], 'L0_ffn_w3': _L0_ffn_in['w3']}
    _x0 = _d['L0_attn_x']
    _d['L0_attn_x'] = jax.random.normal(jax.random.fold_in(jax.random.key(seed), 1), (8, 512, 128), dtype=_x0.dtype)
    del _x0
    return _d

def reference(L0_attn_x, L0_attn_Wq, L0_attn_Wk, L0_attn_Wv, L0_attn_Wo, L0_attn_omega, L0_attn_mu_raw, L0_attn_sigma_raw, L0_attn_eta_raw, L0_attn_gamma_raw, L0_attn_tau, L0_attn_nu_raw, L0_ffn_w_router, L0_ffn_w1, L0_ffn_w2, L0_ffn_w3):

    def _L0_attn_ref(x, Wq, Wk, Wv, Wo, omega, mu_raw, sigma_raw, eta_raw, gamma_raw, tau, nu_raw):
        import jax, jax.numpy as jnp
        import numpy as np
        B, N, DE, H, DH = (2, 128, 128, 16, 64)
        DK = H * DH
        MIN_EXP = -30.0
        EPS = 0.0001
        B_, N_, _ = x.shape
        H_, d_half = omega.shape
        DH_ = 2 * d_half
        DKt = H_ * DH_

        def cproj(W):
            z = x @ W
            D = W.shape[1] // 2
            zc = jax.lax.complex(z[..., :D], z[..., D:])
            return zc.reshape(B_, N_, H_, DH_)
        q, k, v = (cproj(Wq), cproj(Wk), cproj(Wv))
        om = jnp.concatenate([omega, -omega], axis=-1)
        t = jnp.arange(N_, dtype=jnp.float32)
        ang = t[:, None, None] * om[None]
        phase = jax.lax.complex(jnp.cos(ang), jnp.sin(ang))
        qr = q * phase[None]
        kr = k * phase[None]
        mu = jax.nn.sigmoid(mu_raw) + EPS
        dt = jnp.abs(t[:, None] - t[None, :])
        E = jnp.exp(jnp.clip(-mu[:, None, None] * dt[None], MIN_EXP, 0.0))
        s = jnp.einsum('bihd,bjhd->bhij', qr, jnp.conj(kr)).real
        qn = (q.real ** 2 + q.imag ** 2).sum(-1).transpose(0, 2, 1)
        kn = (k.real ** 2 + k.imag ** 2).sum(-1).transpose(0, 2, 1)
        sigma_sq = jax.nn.softplus(sigma_raw)
        eta_sq = jax.nn.softplus(eta_raw)
        gamma_sq = jax.nn.softplus(gamma_raw)
        V = (sigma_sq / (2.0 * mu))[:, None, None] * (1.0 - E * E) + (eta_sq + gamma_sq)[:, None, None]
        maha = jnp.maximum(qn[..., None] + (E * E)[None] * kn[:, :, None, :] - 2.0 * E[None] * s, 0.0) / V[None]
        nu = jax.nn.softplus(nu_raw)
        coef = (-0.5 * tau * (nu + DH_))[None, :, None, None]
        logits = coef * jnp.log1p(maha / nu[None, :, None, None]) - 0.5 * DH_ * jnp.log(V)[None]
        causal = t[:, None] >= t[None, :]
        logits = jnp.where(causal[None, None], logits, -jnp.inf)
        A = jax.nn.softmax(logits, axis=-1)
        out = jnp.einsum('bhij,bjhd->bihd', A.astype(v.dtype), v)
        y = jnp.concatenate([out.real.reshape(B_, N_, DKt), out.imag.reshape(B_, N_, DKt)], axis=-1)
        return y @ Wo

    def _L0_ffn_ref(x, w_router, w1, w2, w3):
        import jax, jax.numpy as jnp
        import numpy as np
        B, S, D = (4, 256, 128)
        E, K = (8, 2)
        H = 176
        bsz, seqlen, dim = x.shape
        xf = x.reshape(-1, dim)
        scores = jax.nn.softmax(xf @ w_router.T, axis=-1)
        expert_weights, expert_indices = jax.lax.top_k(scores, K)
        h = jax.nn.silu(jnp.einsum('td,edh->eth', xf, w1)) * jnp.einsum('td,edh->eth', xf, w3)
        y = jnp.einsum('eth,ehd->etd', h, w2)
        y_t = jnp.swapaxes(y, 0, 1)
        sel = jnp.take_along_axis(y_t, expert_indices[:, :, None], axis=1)
        out = jnp.sum(expert_weights[:, :, None] * sel, axis=1)
        return out.reshape(bsz, seqlen, dim)
    x = L0_attn_x
    x = x + 0.5 * _L0_ffn_ref(_layernorm(x, axis=-1), L0_ffn_w_router, L0_ffn_w1, L0_ffn_w2, L0_ffn_w3)
    x = x + _L0_attn_ref(_layernorm(x, axis=-1), L0_attn_Wq, L0_attn_Wk, L0_attn_Wv, L0_attn_Wo, L0_attn_omega, L0_attn_mu_raw, L0_attn_sigma_raw, L0_attn_eta_raw, L0_attn_gamma_raw, L0_attn_tau, L0_attn_nu_raw)
    x = x + 0.5 * _L0_ffn_ref(_layernorm(x, axis=-1), L0_ffn_w_router, L0_ffn_w1, L0_ffn_w2, L0_ffn_w3)
    return x

_drawn_inputs = setup_inputs


def setup_inputs(seed=0):
    import zlib

    import numpy as np

    out = dict(_drawn_inputs(seed))
    spreads = {'L0_attn_eta_raw': (1.0, 0.6),
     'L0_attn_gamma_raw': (1.0, 0.6),
     'L0_attn_tau': (1.0, 0.2),
     'L0_attn_nu_raw': (4.0, 0.6)}
    factors = {'L0_ffn_w_router': 8.0, 'L0_ffn_w1': 8.0, 'L0_ffn_w2': 8.0, 'L0_ffn_w3': 8.0}
    for name, (base, spread) in spreads.items():
        noise = np.random.default_rng([zlib.crc32(name.encode()), seed]).standard_normal(out[name].shape)
        drawn = base * np.exp(spread * noise) if base else spread * noise
        out[name] = jnp.asarray(drawn.astype(out[name].dtype))
    for name, factor in factors.items():
        out[name] = (out[name] * factor).astype(out[name].dtype)
    return out
```

```python
from contextlib import ExitStack

import numpy as np
import concourse.bass as bass
from concourse import mybir

F32 = mybir.dt.float32
F32R = mybir.dt.float32r
ALU = mybir.AluOpType
ACT = mybir.ActivationFunctionType
AX = mybir.AxisListType

P = 128
D = 128
B, N = 8, 512
TILES = N // P
TT = B * TILES
H, DH = 16, 64
NE, FH = 8, 176
HC = NE * FH // P
LN_EPS = 1e-5
MU_EPS = 1e-4
MIN_EXP = -30.0
MASKED = -1e18
COEF_MIN = 1e-20
LOWEST = -3.0e38
OFF = {0: 0, 2: 128, 3: 512, 1: 1024}
ORDER = (0, 2, 3, 1)
SW = 1280
(NEG_MU, NEG_A, A_PLUS_B, LAM_SCALE, NEG_LN_NU, INV_COEF, COEF, NEG_NU_A, NU_AB, U_MIN) = range(10)
NPAR = 10
TWO_PI_HI, TWO_PI_MID = 6.28125, 0.0019350051879882812
TWO_PI_LO = float(2 * np.pi - TWO_PI_HI - TWO_PI_MID)
ROUND_MAGIC = 12582912.0
PI_BELOW = 3.1415925


def wait(eng, sem, value):
    if not (isinstance(value, int) and value <= 0):
        eng.wait_ge(sem, value)


def apart(eng, passed):
    eng.sem_inc(passed, 1)


def mm3(pe, out, lhs, rhs, start, stop):
    pe.matmul(out, lhs[1], rhs[0], start=start, stop=False)
    pe.matmul(out, lhs[0], rhs[1], start=False, stop=False)
    return pe.matmul(out, lhs[0], rhs[0], start=False, stop=stop)


class Shared:

    def __init__(self, args, out):
        self.x = args["x"]
        self.wqk = args["wqk"]
        self.wv = args["wv"]
        self.wo = args["wo"]
        self.omega = args["omega"]
        self.head_vec = args["head_vec"]
        self.w_router = args["w_router"]
        self.w1 = args["w1"]
        self.w3 = args["w3"]
        self.w2 = args["w2"]
        self.t_row = args["t_row"]
        self.ident_d = args["ident_d"]
        self.dist_d = args["dist_d"]
        self.upper_d = args["upper_d"]
        self.before_d = args["before_d"]
        self.sel = args["sel"]
        self.out = out


def setup_phase(nc, s):
    with ExitStack() as ctx:
        sb = lambda name, shape, dt=F32: ctx.enter_context(nc.sbuf_tensor(name, shape, dt))
        sem = lambda name: ctx.enter_context(nc.semaphore(name))
        w13_raw = sb("w13_raw", [P, 2, HC * P])
        w2_raw = sb("w2_raw", [P, HC * P])
        wr_raw = sb("wr_raw", [P, NE])
        head_in = sb("head_in", [P, 6, H])
        omega = sb("omega", [P, 4])
        t_row = sb("t_row", [P, N])
        ang = sb("ang", [P, 4, N])
        turns = sb("turns", [P, 2, 4, N])
        reduced = sb("reduced", [P, 2, 4, N])
        trig = sb("trig", [P, 3, 4, N])
        wv_raw = sb("wv_raw", [P, 2, P])
        wo_raw = sb("wo_raw", [P, 2, P])
        wvT = sb("wvT", [P, 2, P])
        sc = sb("sc", [P, 16, 4 * H])

        x_in, small_in, ffn_in, cst_in = sem("x_in"), sem("small_in"), sem("ffn_in"), sem("cst_in")
        stats_raw, mv_done = sem("stats_raw"), sem("mv_done")
        hi_done, lo_done = sem("hi_done"), sem("lo_done")
        dve, act = sem("dve_chain"), sem("act_chain")
        angles, trig_done, trig_out = sem("angles"), sem("trig_done"), sem("trig_out")
        wvo_in = [sem("wvo_in0"), sem("wvo_in1")]
        wv_t, wv_sb, wp_mm, wp_hi, wp_lo = (sem(n) for n in ("wv_t", "wv_sb", "wp_mm", "wp_hi", "wp_lo"))
        sm_e, sm_ln = sem("sm_e"), sem("sm_ln")
        stats = sb("stats", [P, TT, 6])

        block = ctx.enter_context(nc.Block())

        @block.sync
        def _(sp):
            x_d = s.x.rearrange("b (i p) d -> p (b i) d", p=P)
            for q in range(4):
                sp.dma_start(s.x_sb[:, q * 8:(q + 1) * 8, :], x_d[:, q * 8:(q + 1) * 8, :]).then_inc(x_in, 16)
            sp.dma_start(head_in[:], s.head_vec.partition_broadcast(P)).then_inc(small_in, 16)
            sp.dma_start(omega[:], s.omega).then_inc(small_in, 16)
            sp.dma_start(t_row[:], s.t_row.partition_broadcast(P)).then_inc(small_in, 16)
            sp.dma_start(w13_raw[:, 0].rearrange("p (e h) -> p e h", e=NE),
                         s.w1.rearrange("e d h -> d e h")).then_inc(ffn_in, 16)
            sp.dma_start(w13_raw[:, 1].rearrange("p (e h) -> p e h", e=NE),
                         s.w3.rearrange("e d h -> d e h")).then_inc(ffn_in, 16)
            sp.dma_start(w2_raw[:].rearrange("p (c n) -> p c n", c=HC),
                         s.w2.rearrange("(c p) n -> p c n", p=P)).then_inc(ffn_in, 16)
            sp.dma_start(wr_raw[:], s.w_router).then_inc(ffn_in, 16)
            sp.dma_start(s.ident[:], s.ident_d).then_inc(cst_in, 16)
            sp.dma_start(s.dist[:], s.dist_d).then_inc(cst_in, 16)
            sp.dma_start(s.upper[:], s.upper_d).then_inc(cst_in, 16)
            sp.dma_start(s.before[:], s.before_d.partition_broadcast(P)).then_inc(cst_in, 16)
            for h in range(2):
                sp.dma_start(wv_raw[:, h], s.wv[h]).then_inc(wvo_in[h], 16)
                sp.dma_start(wo_raw[:, h], s.wo[h]).then_inc(wvo_in[h], 16)
            with nc.sync.Fori(1, H // 2) as i:
                for par in range(2):
                    sp.wait_ge(wp_mm, i * 2 + par - 1)
                    sp.dma_start(wv_raw[:, par], s.wv[i * 2 + par]).then_inc(wvo_in[par], 16)
                    sp.dma_start(wo_raw[:, par], s.wo[i * 2 + par]).then_inc(wvo_in[par], 16)
            sp.wait_ge(trig_done, 3)
            for k in range(3):
                sp.dma_start(s.trig_d[k].rearrange("(g q) d t -> (q d) g t", q=4),
                             trig[:, k]).then_inc(trig_out, 16)
            sp.wait_ge(trig_out, 48)
            sp.wait_ge(cst_in, 64)

        @block.tensor
        def _(pe):
            pe.wait_ge(cst_in, 64)
            with nc.tensor.Fori(0, H // 2) as i:
                for par in range(2):
                    h = i * 2 + par
                    pe.wait_ge(wvo_in[par], i * 32 + 32)
                    pe.wait_ge(wv_sb, h)
                    pe.transpose(s.p6[:, 0:P], wv_raw[:, par], s.ident[:]).then_inc(wv_t, 1)
                    pe.wait_ge(wv_sb, h + 1)
                    pe.wait_ge(wp_lo, h)
                    pe.matmul(s.p7[:, 0:P], wvT[:, par], wo_raw[:, par], start=True, stop=True).then_inc(wp_mm, 1)

        @block.scalar
        def _(a):
            a.wait_ge(ffn_in, 64)
            a.activation(s.w13[0][:], w13_raw[:].rearrange("p a b -> p (a b)"), ACT.Copy).then_inc(hi_done, 1)
            a.activation(s.w2s[0][:], w2_raw[:], ACT.Copy).then_inc(hi_done, 1)
            a.activation(s.wr[0][:], wr_raw[:], ACT.Copy).then_inc(hi_done, 1)
            a.wait_ge(angles, 1)
            a.activation(trig[:, 0], reduced[:, 1], ACT.Sin).then_inc(trig_done, 1)
            a.activation(trig[:, 1], reduced[:, 0], ACT.Sin).then_inc(trig_done, 1)
            a.activation(trig[:, 2], reduced[:, 0], ACT.Sin, scale=-1.0).then_inc(trig_done, 1)
            nc.scalar.preload_act_table_set("natural_log_exp_and_others")
            a.wait_ge(sm_e, 1)
            a.activation(sc[:, 0, 0:H], head_in[:, 0], ACT.Exp, scale=-1.0).then_inc(sm_ln, 1)
            a.activation(sc[:, 2], sc[:, 1], ACT.Exp, scale=-1.0).then_inc(sm_ln, 1)
            a.wait_ge(sm_e, 2)
            a.activation(sc[:, 4], sc[:, 3], ACT.Ln).then_inc(sm_ln, 1)
            a.wait_ge(sm_e, 3)
            a.activation(sc[:, 10, 0:H], sc[:, 8, 3 * H:4 * H], ACT.Ln).then_inc(sm_ln, 1)
            with nc.scalar.Fori(0, H // 2) as i:
                for par in range(2):
                    h = i * 2 + par
                    a.wait_ge(wv_t, h + 1)
                    a.activation(wvT[:, par], s.p6[:, 0:P], ACT.Copy).then_inc(wv_sb, 1)
                    a.wait_ge(wp_mm, h + 1)
                    a.activation(s.wp[0][:, bass.ds(h * P, P)], s.p7[:, 0:P], ACT.Copy).then_inc(wp_hi, 1)

        @block.vector
        def _(v):
            count = [0]

            def step(ins):
                count[0] += 1
                ins.then_inc(dve, 1)
                v.wait_ge(dve, count[0])

            v.wait_ge(small_in, 48)
            for g in range(4):
                last = v.tensor_scalar(ang[:, g], t_row[:], omega[:, g:g + 1], None, ALU.mult)
            step(last)
            for k, quarter in enumerate((0.0, 0.25)):
                step(v.tensor_scalar(turns[:, k], ang[:], float(1 / (2 * np.pi)), quarter, ALU.mult, ALU.add))
                step(v.tensor_scalar(turns[:, k], turns[:, k], ROUND_MAGIC, ROUND_MAGIC, ALU.add, ALU.subtract))
                flat = lambda t: t.rearrange("p g t -> p (g t)")
                src = flat(ang[:])
                for part in (TWO_PI_HI, TWO_PI_MID, TWO_PI_LO):
                    step(v.scalar_tensor_tensor(flat(reduced[:, k]), flat(turns[:, k]), -part, src, ALU.mult, ALU.add))
                    src = flat(reduced[:, k])
                step(v.tensor_scalar(reduced[:, k], reduced[:, k], float(np.pi / 2) * k, PI_BELOW, ALU.add, ALU.min))
                step(v.tensor_scalar(reduced[:, k], reduced[:, k], -PI_BELOW, None, ALU.max))
            v.memset(s.ones[:], 1.0).then_inc(angles, 1)

            raw = head_in[:, 1:5].rearrange("p a h -> p (a h)")
            q = lambda k, j: sc[:, k, j * H:(j + 1) * H]
            ts, tt, stt = v.tensor_scalar, v.tensor_tensor, v.scalar_tensor_tensor
            step(ts(sc[:, 5], raw, -1.0, None, ALU.mult))
            step(tt(sc[:, 1], sc[:, 5], raw, ALU.max))
            v.memset(sc[:, 12], 0.0).then_inc(sm_e, 1)
            v.wait_ge(sm_ln, 2)
            step(ts(sc[:, 3], sc[:, 2], 1.0, None, ALU.add))
            v.memset(sc[:, 13], 0.0).then_inc(sm_e, 1)
            step(ts(sc[:, 5], sc[:, 3], -1.0, None, ALU.add))
            step(ts(sc[:, 6], sc[:, 5], 0.0, None, ALU.is_equal))
            step(tt(sc[:, 5], sc[:, 5], sc[:, 6], ALU.add))
            step(v.reciprocal(sc[:, 7], sc[:, 5]))
            step(tt(sc[:, 7], sc[:, 7], sc[:, 2], ALU.mult))
            v.wait_ge(sm_ln, 3)
            step(tt(sc[:, 7], sc[:, 7], sc[:, 4], ALU.mult))
            step(tt(sc[:, 6], sc[:, 6], sc[:, 2], ALU.mult))
            step(tt(sc[:, 7], sc[:, 7], sc[:, 6], ALU.add))
            step(stt(sc[:, 8], raw, 0.0, sc[:, 7], ALU.max, ALU.add))
            v.memset(sc[:, 14], 0.0).then_inc(sm_e, 1)
            sigma, eta, gamma, nu = (q(8, j) for j in range(4))
            par = lambda k: s.params[:, :, k]
            step(ts(q(9, 0), sc[:, 0, 0:H], 1.0, None, ALU.add))
            step(v.reciprocal(q(9, 1), q(9, 0)))
            step(ts(q(9, 2), q(9, 1), MU_EPS, None, ALU.add))
            step(ts(par(NEG_MU), q(9, 2), -1.0, None, ALU.mult))
            step(v.reciprocal(q(9, 3), q(9, 2)))
            step(tt(q(9, 3), q(9, 3), sigma, ALU.mult))
            step(ts(q(9, 3), q(9, 3), 0.5, None, ALU.mult))
            step(ts(par(NEG_A), q(9, 3), -1.0, None, ALU.mult))
            step(tt(q(11, 0), eta, gamma, ALU.add))
            step(tt(par(A_PLUS_B), q(11, 0), q(9, 3), ALU.add))
            step(tt(par(NEG_NU_A), par(NEG_A), nu, ALU.mult))
            step(tt(par(NU_AB), par(A_PLUS_B), nu, ALU.mult))
            step(tt(par(U_MIN), q(11, 0), nu, ALU.mult))
            step(ts(q(11, 1), nu, float(DH), -0.5, ALU.add, ALU.mult))
            step(tt(q(11, 1), q(11, 1), head_in[:, 5], ALU.mult))
            step(ts(q(11, 2), q(11, 1), -1.0, None, ALU.mult))
            step(tt(q(11, 2), q(11, 2), q(11, 1), ALU.max))
            step(ts(q(11, 2), q(11, 2), COEF_MIN, -COEF_MIN, ALU.is_lt, ALU.mult))
            step(ts(q(11, 3), q(11, 2), 1.0 / COEF_MIN, 1.0, ALU.mult, ALU.add))
            step(tt(q(11, 1), q(11, 1), q(11, 3), ALU.mult))
            step(tt(par(COEF), q(11, 1), q(11, 2), ALU.add))
            step(v.reciprocal(par(INV_COEF), par(COEF)))
            step(ts(par(LAM_SCALE), par(INV_COEF), -0.5 * DH, -1.0, ALU.mult, ALU.add))
            v.wait_ge(sm_ln, 4)
            step(ts(par(NEG_LN_NU), sc[:, 10, 0:H], -1.0, None, ALU.mult))

            for k, (whole, pair) in enumerate(((w13_raw[:].rearrange("p a b -> p (a b)"), s.w13),
                                               (w2_raw[:], s.w2s), (wr_raw[:], s.wr))):
                v.wait_ge(hi_done, k + 1)
                v.tensor_tensor(pair[1][:], whole, pair[0][:].bitcast(F32), ALU.subtract).then_inc(lo_done, 1)

            v.wait_ge(x_in, 64)
            for t in range(TT):
                last = v.bn_stats(stats[:, t, :], s.x_sb[:, t, :])
            last.then_inc(stats_raw, 1)
            v.wait_ge(stats_raw, 1)
            for t in range(TT):
                v.bn_aggr(s.mv[:, t, :], stats[:, t, :]).then_inc(mv_done, 1)

            with nc.vector.Fori(0, H) as h:
                v.wait_ge(wp_hi, h + 1)
                v.tensor_tensor(s.wp[1][:, bass.ds(h * P, P)], s.p7[:, 0:P],
                                s.wp[0][:, bass.ds(h * P, P)].bitcast(F32), ALU.subtract).then_inc(wp_lo, 1)


def norm_phase(nc, s, tag, route):
    with ExitStack() as ctx:
        sb = lambda name, shape, dt=F32: ctx.enter_context(nc.sbuf_tensor(f"{name}_{tag}", shape, dt))
        sem = lambda name: ctx.enter_context(nc.semaphore(f"{name}_{tag}"))
        var = sb("var", [P, TT])
        root = sb("root", [P, TT])
        rstd = sb("rstd", [P, TT])
        tmp = sb("tmp", [P, TT])
        shift = sb("shift", [P, TT])
        xn = sb("xn", [P, 2, TILES, P])
        dve, root_done = sem("dve_chain"), sem("root_done")
        var_done, xn_done, xt_done, xhi_done, xlo_done = (sem(n) for n in (
            "var_done", "xn_done", "xt_done", "xhi_done", "xlo_done"))
        logit_done, score_in, exp_done, w_done, wt_done, wt_copied = (sem(n) for n in (
            "logit_done", "score_in", "exp_done", "w_done", "wt_done", "wt_copied"))
        if route:
            e_s = sb("e_s", [P, TT, NE])
            sm = sb("sm", [P, 3, TT])
            gt = sb("gt", [P, TT, NE, NE])
            eq = sb("eq", [P, TT, NE, NE])
            hi_r = sb("hi_r", [P, TT, NE], F32R)
            w16 = sb("w16", [P, TT, 2 * NE])
            sel_raw = sb("sel_raw", [2 * NE, HC * P])
            sel_in, sel_done = sem("sel_in"), sem("sel_done")
        banks = (s.pS[:, 0:N], s.pS[:, N:2 * N])
        logits = s.p7[:, 0:TT * NE].rearrange("p (t e) -> p t e", e=NE)
        flat = lambda t: t.rearrange("p a b -> p (a b)")
        block = ctx.enter_context(nc.Block())

        if route:
            @block.sync
            def _(sp):
                sp.dma_start(sel_raw[:], s.sel).then_inc(sel_in, 16)

        @block.tensor
        def _(pe):
            with nc.tensor.Fori(0, B // 2) as i:
                for par in range(2):
                    pe.wait_ge(xn_done, i * 2 + par + 1)
                    pe.wait_ge(xlo_done, i * 2 + (par - 1 if par else 0)) if par else pe.wait_ge(xlo_done, i * 2)
                    for k in range(TILES):
                        last = pe.transpose(banks[par][:, k * P:(k + 1) * P], xn[:, par, k], s.ident[:])
                    last.then_inc(xt_done, 1)
            if route:
                for t in range(TT):
                    if t % TILES == 0:
                        pe.wait_ge(xlo_done, t // TILES + 1)
                    cols = slice(t * P, (t + 1) * P)
                    last = mm3(pe, logits[:, t], (s.xT[0][:, cols], s.xT[1][:, cols]),
                               (s.wr[0][:], s.wr[1][:]), True, True)
                last.then_inc(logit_done, 1)
                pe.wait_ge(w_done, 1)
                for c in range(B):
                    if c >= 2:
                        pe.wait_ge(wt_copied, c - 1)
                    for k in range(TILES):
                        last = pe.transpose(banks[c % 2][0:2 * NE, k * P:(k + 1) * P],
                                            w16[:, c * TILES + k, :], s.ident[:])
                    last.then_inc(wt_done, 1)

        @block.scalar
        def _(a):
            a.wait_ge(var_done, 1)
            a.activation(root[:], var[:], ACT.Sqrt).then_inc(root_done, 1)
            nc.scalar.preload_act_table_set("natural_log_exp_and_others")
            with nc.scalar.Fori(0, B // 2) as i:
                for par in range(2):
                    a.wait_ge(xt_done, i * 2 + par + 1)
                    a.activation(s.xT[0][:, bass.ds((i * 2 + par) * N, N)], banks[par], ACT.Copy).then_inc(xhi_done, 1)
            if route:
                a.wait_ge(sel_in, 16)
                a.activation(s.selr[:], sel_raw[:], ACT.Copy).then_inc(sel_done, 1)
                a.wait_ge(score_in, 1)
                a.activation(e_s[:], e_s[:], ACT.Exp).then_inc(exp_done, 1)
                for c in range(B):
                    a.wait_ge(wt_done, c + 1)
                    a.activation(s.wT[:, c * N:(c + 1) * N], banks[c % 2][0:2 * NE, :], ACT.Copy).then_inc(wt_copied, 1)

        @block.vector
        def _(v):
            count = [0]

            def step(ins):
                count[0] += 1
                ins.then_inc(dve, 1)
                v.wait_ge(dve, count[0])

            v.tensor_scalar(var[:], s.mv[:, :, 1], LN_EPS, None, ALU.add).then_inc(var_done, 1)
            v.wait_ge(root_done, 1)
            step(v.reciprocal(rstd[:], root[:]))
            step(v.tensor_tensor(tmp[:], rstd[:], rstd[:], ALU.mult))
            step(v.tensor_tensor(tmp[:], tmp[:], var[:], ALU.mult))
            step(v.tensor_scalar(tmp[:], tmp[:], -0.5, 1.5, ALU.mult, ALU.add))
            step(v.tensor_tensor(rstd[:], rstd[:], tmp[:], ALU.mult))
            def normalise(i, par):
                for k in range(TILES):
                    t = (i * 2 + par) * TILES + k
                    last = v.tensor_scalar(xn[:, par, k], s.x_sb[:, bass.ds(t, 1), :].rearrange("p a d -> p (a d)"),
                                           s.mv[:, bass.ds(t, 1), 0], rstd[:, bass.ds(t, 1)],
                                           ALU.subtract, ALU.mult)
                last.then_inc(xn_done, 1)

            def low(i, par):
                v.wait_ge(xhi_done, i * 2 + par + 1)
                cols = bass.ds((i * 2 + par) * N, N)
                v.tensor_tensor(s.xT[1][:, cols], banks[par], s.xT[0][:, cols].bitcast(F32),
                                ALU.subtract).then_inc(xlo_done, 1)

            with nc.vector.Fori(0, B // 2) as i:
                for par in range(2):
                    v.wait_ge(xt_done, i * 2)
                    normalise(i, par)
                for par in range(2):
                    low(i, par)
            if route:
                v.wait_ge(logit_done, 1)
                wide = lambda t: t.unsqueeze(2).broadcast_to([P, TT, NE])
                step(v.tensor_reduce(sm[:, 0], logits, AX.X, ALU.max))
                v.tensor_tensor(e_s[:], logits, wide(sm[:, 0]), ALU.subtract).then_inc(score_in, 1)
                v.wait_ge(exp_done, 1)
                step(v.tensor_reduce(sm[:, 1], e_s[:], AX.X, ALU.add))
                step(v.reciprocal(sm[:, 2], sm[:, 1]))
                step(v.tensor_tensor(e_s[:], e_s[:], wide(sm[:, 2]), ALU.mult))
                by_f = e_s[:].unsqueeze(2).broadcast_to([P, TT, NE, NE])
                by_e = e_s[:].unsqueeze(3).broadcast_to([P, TT, NE, NE])
                before = s.before[:].unsqueeze(1).broadcast_to([P, TT, NE * NE])
                step(v.tensor_tensor(gt[:], by_f, by_e, ALU.is_gt))
                step(v.tensor_tensor(eq[:], by_f, by_e, ALU.is_equal))
                v3 = lambda t: t.rearrange("p t e f -> p t (e f)")
                step(v.tensor_tensor(v3(eq[:]), v3(eq[:]), before, ALU.mult))
                step(v.tensor_tensor(flat(v3(gt[:])), flat(v3(gt[:])), flat(v3(eq[:])), ALU.add))
                rank = eq[:, :, 0, :]
                step(v.tensor_reduce(rank, gt[:], AX.X, ALU.add))
                step(v.scalar_tensor_tensor(e_s[:], rank, 2.0, e_s[:], ALU.is_lt, ALU.mult))
                step(v.tensor_copy(hi_r[:], e_s[:]))
                step(v.tensor_copy(w16[:, :, 0:NE], hi_r[:].bitcast(F32)))
                v.tensor_tensor(w16[:, :, NE:2 * NE], e_s[:], hi_r[:].bitcast(F32),
                                ALU.subtract).then_inc(w_done, 1)


def ffn_phase(nc, s, tag, last_phase):
    with ExitStack() as ctx:
        sb = lambda name, shape, dt=F32: ctx.enter_context(nc.sbuf_tensor(f"{name}_{tag}", shape, dt))
        sem = lambda name: ctx.enter_context(nc.semaphore(f"{name}_{tag}"))
        silu = sb("silu", [P, 2, N])
        gated = sb("gated", [P, 2, N])
        hid = sb("hid", [P, 2, N])
        hid_hi = sb("hid_hi", [P, 2, N], F32R)
        hid_lo = sb("hid_lo", [P, 2, N], F32R)
        yT = sb("yT", [P, N])
        stats = sb("stats", [P, TILES, 6])
        mean_var = sb("mean_var", [P, TILES, 2])
        aggr_done, pe_passed, dve_passed = sem("aggr_done"), sem("pe_passed"), sem("dve_passed")
        guw_done, silu_done, gated_done, hid_done, hi_done, lo_done = (sem(n) for n in (
            "guw_done", "silu_done", "gated_done", "hid_done", "hi_done", "lo_done"))
        y_slot, y_out, y_turned, x_done, stat_done, stored = (sem(n) for n in (
            "y_slot", "y_out", "y_turned", "x_done", "stat_done", "stored"))
        g_bank = (s.pS[:, 0:N], s.pQK[:, 0:N])
        u_bank = (s.pS[:, N:2 * N], s.pQK[:, N:2 * N])
        w_bank = (s.pS[:, 2 * N:3 * N], s.p5[:])
        y_bank, t_bank = s.p6[:], s.p7[:]
        SLOTS = 2 * HC
        block = ctx.enter_context(nc.Block())

        def slots(eng, body):
            with eng.Fori(0, B // 2 - 1) as i:
                for u in range(SLOTS):
                    body(i, u, False)
            for u in range(SLOTS):
                body(B // 2 - 1, u, True)

        @block.tensor
        def _(pe):
            def products(i, u):
                e, k, c, par = i * SLOTS + u, u % HC, i * 2 + u // HC, u % 2
                hid_cols = slice(k * P, (k + 1) * P)
                up_cols = slice((HC + k) * P, (HC + k + 1) * P)
                toks = bass.ds(c * N, N)
                xT = (s.xT[0][:, toks], s.xT[1][:, toks])
                wait(pe, silu_done, e - 1)
                mm3(pe, g_bank[par], tuple(w[:, hid_cols] for w in s.w13), xT, True, True)
                wait(pe, gated_done, e - 1)
                mm3(pe, u_bank[par], tuple(w[:, up_cols] for w in s.w13), xT, True, True)
                wait(pe, hid_done, e - 1)
                apart(pe, pe_passed)
                pe.matmul(w_bank[par], s.selr[:, hid_cols], s.wT[:, toks],
                          start=True, stop=True).then_inc(guw_done, 1)

            products(0, 0)
            products(0, 1)

            def body(i, u, end):
                e, k, c, par = i * SLOTS + u, u % HC, i * 2 + u // HC, u % 2
                if not (end and u + 2 >= SLOTS):
                    products(i + (u + 2) // SLOTS if u + 2 >= SLOTS else i, (u + 2) % SLOTS)
                pe.wait_ge(lo_done, e + 1)
                if k == 0:
                    wait(pe, y_out, c)
                mm3(pe, y_bank, tuple(w[:, k * P:(k + 1) * P] for w in s.w2s),
                    (hid_hi[:, par], hid_lo[:, par]), k == 0, k == HC - 1).then_inc(y_slot, 1)

            def turn(c):
                pe.wait_ge(y_out, c + 1)
                wait(pe, x_done, c)
                for k in range(TILES):
                    last = pe.transpose(t_bank[:, k * P:(k + 1) * P], yT[:, k * P:(k + 1) * P], s.ident[:])
                last.then_inc(y_turned, 1)

            def chunked(i, u, end):
                body(i, u, end)
                if u % HC == HC - 1:
                    turn(i * 2 + u // HC)

            slots(nc.tensor, chunked)

        @block.scalar
        def _(a):
            def do_silu(i, u):
                e, par = i * SLOTS + u, u % 2
                a.wait_ge(guw_done, e + 1)
                wait(a, gated_done, e - 1)
                a.activation(silu[:, par], g_bank[par], ACT.Silu).then_inc(silu_done, 1)

            def body(i, u, end):
                e, par = i * SLOTS + u, u % 2
                if not (end and u + 1 == SLOTS):
                    do_silu(i + 1 if u + 1 == SLOTS else i, (u + 1) % SLOTS)
                a.wait_ge(hid_done, e + 1)
                wait(a, y_slot, e - (u > 0))
                a.activation(hid_hi[:, par], hid[:, par], ACT.Copy).then_inc(hi_done, 1)
                if u % HC == HC - 1:
                    c = i * 2 + u // HC
                    a.wait_ge(y_slot, e + 1)
                    wait(a, y_turned, c)
                    a.activation(yT[:], y_bank, ACT.Copy, scale=0.5).then_inc(y_out, 1)

            do_silu(0, 0)
            slots(nc.scalar, body)

        @block.vector
        def _(v):
            def gate(i, u):
                e, par = i * SLOTS + u, u % 2
                v.wait_ge(silu_done, e + 1)
                v.tensor_tensor(gated[:, par], u_bank[par], silu[:, par], ALU.mult).then_inc(gated_done, 1)

            def body(i, u, end):
                e, par, c = i * SLOTS + u, u % 2, i * 2 + u // HC
                v.wait_ge(gated_done, e + 1)
                v.tensor_tensor(hid[:, par], w_bank[par], gated[:, par], ALU.mult).then_inc(hid_done, 1)
                if not (end and u + 1 == SLOTS):
                    gate(i + 1 if u + 1 == SLOTS else i, (u + 1) % SLOTS)
                v.wait_ge(hi_done, e + 1)
                wait(v, y_slot, e - (u > 0))
                v.tensor_tensor(hid_lo[:, par], hid[:, par], hid_hi[:, par].bitcast(F32),
                                ALU.subtract).then_inc(lo_done, 1)
                if u % HC == HC - 1:
                    add(c)

            def add(c):
                v.wait_ge(y_turned, c + 1)
                xc = s.x_sb[:, bass.ds(c * TILES, TILES), :]
                v.tensor_tensor(xc, t_bank.rearrange("p (a b) -> p a b", a=TILES), xc, ALU.add).then_inc(x_done, 1)
                if not last_phase:
                    v.wait_ge(x_done, c + 1)
                    apart(v, dve_passed)
                    for k in range(TILES):
                        last = v.bn_stats(stats[:, k, :],
                                          s.x_sb[:, bass.ds(c * TILES + k, 1), :].rearrange("p a d -> p (a d)"))
                    last.then_inc(stat_done, 1)
                    v.wait_ge(stat_done, c + 1)
                    apart(v, dve_passed)
                    for k in range(TILES):
                        last = v.bn_aggr(mean_var[:, k, :], stats[:, k, :])
                    last.then_inc(aggr_done, 1)
                    v.wait_ge(aggr_done, c + 1)
                    v.tensor_copy(s.mv[:, bass.ds(c * TILES, TILES), :], mean_var[:])

            gate(0, 0)
            slots(nc.vector, body)

        if last_phase:
            @block.sync
            def _(sp):
                for c in range(B):
                    sp.wait_ge(x_done, c + 1)
                    sp.dma_start(s.out.rearrange("b (i p) d -> p b i d", p=P)[:, c],
                                 s.x_sb[:, c * TILES:(c + 1) * TILES, :]).then_inc(stored, 16)
                sp.wait_ge(stored, 16 * B)


def attention_phase(nc, s):
    PAIRS = H * B
    with ExitStack() as ctx:
        sb = lambda name, shape, dt=F32: ctx.enter_context(nc.sbuf_tensor(name, shape, dt))
        sem = lambda name: ctx.enter_context(nc.semaphore(name))
        decay = [sb(f"decay{k}", [P, SW]) for k in range(2)]
        decay2 = [sb(f"decay2_{k}", [P, SW]) for k in range(2)]
        lam = [sb(f"lam{k}", [P, SW]) for k in range(2)]
        cos = [sb(f"cos{k}", [P, N]) for k in range(2)]
        sin = [sb(f"sin{k}", [P, N]) for k in range(2)]
        hp = [sb(f"hp{k}", [P, NPAR]) for k in range(2)]
        wqk_raw = sb("wqk_raw", [P, 2 * P])
        wqk = [[sb(f"wqk_{half}{k}", [P, 2 * P], F32R) for half in ("hi", "lo")] for k in range(2)]
        swapped = sb("swapped", [P, 2 * N])
        by_cos = sb("by_cos", [P, 2 * N])
        by_sin = sb("by_sin", [P, 2 * N])
        squares = sb("squares", [P, 2 * N])
        rot = [sb(f"rot{k}", [P, 2 * N]) for k in range(2)]
        knorm = sb("knorm", [P, N])
        qnorm = sb("qnorm", [P, 2, TILES])
        ek = [sb(f"ek{k}", [P, SW]) for k in range(2)]
        u = sb("u", [P, SW])
        z = sb("z", [P, SW])
        probT = sb("probT", [P, SW])
        val = [sb(f"val{k}", [P, N]) for k in range(2)]
        zmax = sb("zmax", [P, TILES])
        nmax = sb("nmax", [P, TILES])
        rsum = sb("rsum", [P, 2, TILES])
        rinv = sb("rinv", [P, 2, TILES])
        stats = sb("stats_at", [P, TT, 6])
        names = ("w_in trig_in0 trig_in1 w_hi w_lo hp_done arg_done decay_done decay2_done lnv_done lam0_done "
                 "lam_done qk_done swap_done cos_done sin_done sq_done rot_done norm_done qn_done kn_done "
                 "ek_done s_done es_done sum_done u_done ln_done zred_done nmax_done exp_done v_done "
                 "val_done tr_done trc_done av_done rinv_done acc_done stat_done dve_passed pool_passed")
        S = {n: sem(n) for n in names.split()}
        trig_in = (S["trig_in0"], S["trig_in1"])
        block = ctx.enter_context(nc.Block())

        def steps(eng, a_step):
            a_step(0, -2, False)
            a_step(0, -1, False)
            with eng.Fori(0, H // 2 - 1) as i:
                for k in range(16):
                    a_step(i, k, False)
            for k in range(16):
                a_step(H // 2 - 1, k, True)

        def stages(k, end):
            return k >= 0, -1 <= k and not (end and k + 1 >= 16), not (end and k + 2 >= 16)

        def head_built(k, end):
            if k == 2:
                return 1
            if k == 10 and not end:
                return 2
            return None

        @block.sync
        def _(sp):
            def load(i, off):
                h, par = i * 2 + off, off % 2
                wait(sp, S["w_lo"], h)
                sp.dma_start(wqk_raw[:], s.wqk[h]).then_inc(S["w_in"], 16)
                wait(sp, S["sin_done"], (i * 2 + off - 1) * B)
                wait(sp, S["cos_done"], (i * 2 + off - 1) * B)
                for g in range(4):
                    rows = slice(32 * g, 32 * g + 32)
                    sp.dma_start(cos[par][rows, :], s.trig_d[0, h]).then_inc(trig_in[par], 16)
                    which = (2, 1, 1, 2)[g]
                    sp.dma_start(sin[par][rows, :], s.trig_d[which, h]).then_inc(trig_in[par], 16)

            load(0, 0)
            with nc.sync.Fori(0, H // 2 - 1) as i:
                load(i, 1)
                load(i, 2)
            load(H // 2 - 1, 1)

        @block.tensor
        def _(pe):
            def a_step(i, k, end):
                n = i * 16 + k
                out, score, proj = stages(k, end)
                if proj:
                    c, par, b = n + 2, ((k + 2) // B) % 2, (k + 2) % B
                    head = i * 2 + (k + 2) // B
                    wait(pe, S["w_hi"], head + 1)
                    wait(pe, S["w_lo"], head + 1)
                    wait(pe, S["swap_done"], c)
                    wait(pe, S["cos_done"], c)
                    wait(pe, S["norm_done"], c)
                    wait(pe, S["qn_done"], c)
                    toks = slice(b * N, (b + 1) * N)
                    for j in range(2):
                        last = mm3(pe, s.pQK[:, j * N:(j + 1) * N],
                                   tuple(w[:, j * P:(j + 1) * P] for w in wqk[par]),
                                   (s.xT[0][:, toks], s.xT[1][:, toks]), True, True)
                    last.then_inc(S["qk_done"], 1)
                if score:
                    m, par, b = n + 1, ((k + 1) // B) % 2, (k + 1) % B
                    head = i * 2 + (k + 1) // B
                    wait(pe, S["rot_done"], m + 1)
                    wait(pe, S["es_done"], m)
                    r = rot[(k + 1) % 2]
                    for I in ORDER:
                        last = pe.matmul(s.pS[:, OFF[I]:OFF[I] + (I + 1) * P], r[:, I * P:(I + 1) * P],
                                         r[:, N:N + (I + 1) * P], start=True, stop=True)
                    last.then_inc(S["s_done"], 1)
                    wait(pe, S["val_done"], m)
                    wo = tuple(w[:, bass.ds(head * P, P)] for w in s.wp)
                    for J in range(TILES):
                        t = slice((b * TILES + J) * P, (b * TILES + J + 1) * P)
                        last = mm3(pe, s.p5[:, J * P:(J + 1) * P], (s.xT[0][:, t], s.xT[1][:, t]), wo, True, True)
                    last.then_inc(S["v_done"], 1)
                if out:
                    def turn(r):
                        wait(pe, S["trc_done"], n * 3 + r)
                        for col in range(r * N, min((r + 1) * N, SW), P):
                            last = pe.transpose(s.p6[:, col - r * N:col - r * N + P], z[:, col:col + P], s.ident[:])
                        last.then_inc(S["tr_done"], 1)

                    def average(tiles):
                        for I in tiles:
                            for J in range(I + 1):
                                last = pe.matmul(s.p7[:, I * P:(I + 1) * P],
                                                 probT[:, OFF[I] + J * P:OFF[I] + (J + 1) * P],
                                                 val[k % 2][:, J * P:(J + 1) * P], start=(J == 0), stop=(J == I))
                        return last

                    wait(pe, S["exp_done"], n + 1)
                    turn(0)
                    turn(1)
                    wait(pe, S["val_done"], n + 1)
                    wait(pe, S["acc_done"], n)
                    average((0, 2))
                    turn(2)
                    wait(pe, S["trc_done"], n * 3 + 2)
                    average((3,))
                    wait(pe, S["trc_done"], n * 3 + 3)
                    average((1,)).then_inc(S["av_done"], 1)
                if proj:
                    wait(pe, S["sq_done"], c + 1)
                    wait(pe, S["swap_done"], c + 1)
                    wait(pe, S["cos_done"], c + 1)
                    pe.matmul(s.pQK[:, 0:N], s.ones[:], squares[:, N:2 * N], start=True, stop=True)
                    for I in range(TILES):
                        last = pe.matmul(s.pQK[:, N + I:N + I + 1], squares[:, I * P:(I + 1) * P],
                                         s.ones[:, 0:1], start=True, stop=True)
                    last.then_inc(S["kn_done"], 1)

            steps(nc.tensor, a_step)

        @block.scalar
        def _(a):
            def build(i, off):
                h, par = i * 2 + off, off % 2
                a.wait_ge(S["w_in"], h * 16 + 16)
                wait(a, S["qk_done"], (i * 2 + off - 1) * B)
                a.activation(wqk[par][0][:], wqk_raw[:], ACT.Copy).then_inc(S["w_hi"], 1)
                a.wait_ge(S["arg_done"], h + 1)
                a.activation(decay[par][:], decay[par][:], ACT.Exp).then_inc(S["decay_done"], 1)
                a.wait_ge(S["decay_done"], h + 1)
                wait(a, S["ek_done"], (i * 2 + off - 1) * B)
                a.activation(decay2[par][:], decay[par][:], ACT.Square).then_inc(S["decay2_done"], 1)
                a.wait_ge(S["decay2_done"], h + 1)
                a.activation(lam[par][:], decay2[par][:], ACT.Ln, bias=hp[par][:, A_PLUS_B:A_PLUS_B + 1],
                             scale=hp[par][:, NEG_A:NEG_A + 1]).then_inc(S["lnv_done"], 1)

            def a_step(i, k, end):
                n = i * 16 + k
                out, score, proj = stages(k, end)
                if out:
                    a.wait_ge(S["nmax_done"], n + 1)
                    for I in ORDER:
                        cols = slice(OFF[I], OFF[I] + (I + 1) * P)
                        last = a.activation(z[:, cols], z[:, cols], ACT.Exp, bias=nmax[:, I:I + 1],
                                            accum_out=rsum[:, k % 2, I:I + 1])
                    last.then_inc(S["exp_done"], 1)
                if proj:
                    c = n + 2
                    wait(a, S["cos_done"], c + 1)
                    wait(a, S["sin_done"], c)
                    wait(a, S["sq_done"], c)
                    a.activation(swapped[0:DH, :], s.pQK[DH:P, :], ACT.Copy)
                    a.activation(swapped[DH:P, :], s.pQK[0:DH, :], ACT.Copy).then_inc(S["swap_done"], 1)
                if out:
                    for r in range(3):
                        a.wait_ge(S["tr_done"], n * 3 + r + 1)
                        wait(a, S["av_done"], n)
                        w = min(N, SW - r * N)
                        a.activation(probT[:, r * N:r * N + w], s.p6[:, 0:w], ACT.Copy).then_inc(S["trc_done"], 1)
                if score:
                    m = n + 1
                    wait(a, S["v_done"], m + 1)
                    wait(a, S["av_done"], m - 1)
                    a.activation(val[(k + 1) % 2][:], s.p5[:], ACT.Copy).then_inc(S["val_done"], 1)
                    wait(a, S["u_done"], m + 1)
                    a.activation(u[:], u[:], ACT.Ln).then_inc(S["ln_done"], 1)
                if proj:
                    par = ((k + 2) // B) % 2
                    wait(a, S["kn_done"], c + 1)
                    wait(a, S["ek_done"], c)
                    a.activation(knorm[:], s.pQK[:, 0:N], ACT.Identity,
                                 bias=hp[par][:, NEG_NU_A:NEG_NU_A + 1]).then_inc(S["norm_done"], 1)
                if head_built(k, end):
                    build(i, head_built(k, end))

            nc.scalar.preload_act_table_set("natural_log_exp_and_others")
            build(0, 0)
            steps(nc.scalar, a_step)

        @block.gpsimd
        def _(g):
            def build(i, off):
                h, par = i * 2 + off, off % 2
                g.wait_ge(S["lnv_done"], h + 1)
                apart(g, S["pool_passed"])
                g.tensor_scalar(lam[par][:], lam[par][:], hp[par][:, LAM_SCALE:LAM_SCALE + 1],
                                hp[par][:, NEG_LN_NU:NEG_LN_NU + 1], ALU.mult, ALU.add).then_inc(S["lam0_done"], 1)

            def a_step(i, k, end):
                n = i * 16 + k
                proj = stages(k, end)[2]
                if proj:
                    c, par = n + 2, ((k + 2) // B) % 2
                    wait(g, S["swap_done"], c + 1)
                    wait(g, S["kn_done"], c)
                    g.tensor_tensor(squares[:], swapped[:], swapped[:], ALU.mult).then_inc(S["sq_done"], 1)
                    wait(g, S["cos_done"], c + 1)
                    wait(g, S["sin_done"], c + 1)
                    wait(g, S["s_done"], c - 1)
                    g.tensor_tensor(rot[k % 2][:], by_cos[:], by_sin[:], ALU.add).then_inc(S["rot_done"], 1)
                    wait(g, S["decay2_done"], i * 2 + (k + 2) // B + 1)
                    wait(g, S["norm_done"], c + 1)
                    wait(g, S["sum_done"], c - 1)
                    for I in ORDER:
                        cols = slice(OFF[I], OFF[I] + (I + 1) * P)
                        last = g.tensor_tensor(ek[k % 2][:, cols], decay2[par][:, cols], knorm[:, 0:(I + 1) * P],
                                               ALU.mult)
                    last.then_inc(S["ek_done"], 1)
                if head_built(k, end):
                    build(i, head_built(k, end))

            build(0, 0)
            steps(nc.gpsimd, a_step)

        @block.vector
        def _(v):
            def build_front(i, off):
                h, par = i * 2 + off, off % 2
                wait(v, S["norm_done"], (i * 2 + off - 1) * B)
                v.tensor_copy(hp[par][:], s.params[:, bass.ds(h, 1), :].rearrange("p a c -> p (a c)")).then_inc(S["hp_done"], 1)
                v.wait_ge(S["hp_done"], h + 1)
                v.tensor_scalar(decay[par][:], s.dist[:], hp[par][:, NEG_MU:NEG_MU + 1], MIN_EXP,
                                ALU.mult, ALU.max).then_inc(S["arg_done"], 1)
                v.wait_ge(S["w_hi"], h + 1)
                wait(v, S["qk_done"], (i * 2 + off - 1) * B)
                v.tensor_tensor(wqk[par][1][:], wqk_raw[:], wqk[par][0][:].bitcast(F32),
                                ALU.subtract).then_inc(S["w_lo"], 1)

            def build_back(i, off):
                h, par = i * 2 + off, off % 2
                v.wait_ge(S["lam0_done"], h + 1)
                for I in range(TILES):
                    cols = slice(OFF[I] + I * P, OFF[I] + (I + 1) * P)
                    last = v.scalar_tensor_tensor(lam[par][:, cols], s.upper[:], hp[par][:, INV_COEF:INV_COEF + 1],
                                                  lam[par][:, cols], ALU.mult, ALU.add)
                last.then_inc(S["lam_done"], 1)

            def accumulate(k, n):
                b = k % B
                v.wait_ge(S["av_done"], n + 1)
                v.wait_ge(S["rinv_done"], n + 1)
                for I in range(TILES):
                    xt = s.x_sb[:, b * TILES + I, :]
                    last = v.scalar_tensor_tensor(xt, s.p7[:, I * P:(I + 1) * P], rinv[:, k % 2, I:I + 1], xt,
                                                  ALU.mult, ALU.add)
                last.then_inc(S["acc_done"], 1)

            def a_step(i, k, end):
                n = i * 16 + k
                out, score, proj = stages(k, end)
                if out:
                    par = (k // B) % 2
                    head = i * 2 + k // B
                    v.wait_ge(S["ln_done"], n + 1)
                    v.wait_ge(S["lam_done"], head + 1)
                    wait(v, S["exp_done"], n)
                    wait(v, S["tr_done"], n * 3)
                    apart(v, S["dve_passed"])
                    for I in ORDER:
                        cols = slice(OFF[I], OFF[I] + (I + 1) * P)
                        last = v.tensor_tensor_reduce(z[:, cols], u[:, cols], lam[par][:, cols],
                                                      hp[par][:, COEF:COEF + 1], LOWEST, ALU.add, ALU.max,
                                                      zmax[:, I:I + 1])
                    last.then_inc(S["zred_done"], 1)
                    v.wait_ge(S["zred_done"], n + 1)
                    v.tensor_scalar(nmax[:], zmax[:], -1.0, None, ALU.mult).then_inc(S["nmax_done"], 1)
                if proj:
                    c, par = n + 2, ((k + 2) // B) % 2
                    head = i * 2 + (k + 2) // B
                    both = lambda t: t[:].unsqueeze(1).broadcast_to([P, 2, N])
                    two = lambda t: t.rearrange("p (a t) -> p a t", a=2)
                    wait(v, trig_in[par], i * 128 + ((k + 2) // (2 * B) + 1) * 128)
                    wait(v, S["qk_done"], c + 1)
                    wait(v, S["rot_done"], c)
                    v.tensor_tensor(two(by_cos[:]), two(s.pQK[:]), both(cos[par]), ALU.mult).then_inc(S["cos_done"], 1)
                if score:
                    m, par = n + 1, ((k + 1) // B) % 2
                    wait(v, S["decay_done"], i * 2 + (k + 1) // B + 1)
                    wait(v, S["s_done"], m + 1)
                    wait(v, S["zred_done"], m)
                    v.scalar_tensor_tensor(u[:], s.pS[:, 0:SW], -2.0, decay[par][:], ALU.mult,
                                           ALU.mult).then_inc(S["es_done"], 1)
                if proj:
                    par = ((k + 2) // B) % 2
                    wait(v, S["swap_done"], c + 1)
                    v.tensor_tensor(two(by_sin[:]), two(swapped[:]), both(sin[par]), ALU.mult).then_inc(S["sin_done"], 1)
                if score:
                    par = ((k + 1) // B) % 2
                    wait(v, S["ek_done"], m + 1)
                    wait(v, S["es_done"], m + 1)
                    v.tensor_tensor(u[:], u[:], ek[(k + 1) % 2][:], ALU.add).then_inc(S["sum_done"], 1)
                    wait(v, S["sum_done"], m + 1)
                    wait(v, S["qn_done"], m + 1)
                    for I in ORDER:
                        cols = slice(OFF[I], OFF[I] + (I + 1) * P)
                        last = v.tensor_scalar(u[:, cols], u[:, cols], qnorm[:, (k + 1) % 2, I:I + 1],
                                               hp[par][:, U_MIN:U_MIN + 1], ALU.add, ALU.max)
                    last.then_inc(S["u_done"], 1)
                if out:
                    v.wait_ge(S["exp_done"], n + 1)
                    v.reciprocal(rinv[:, k % 2, :], rsum[:, k % 2, :]).then_inc(S["rinv_done"], 1)
                    accumulate(k, n)
                if proj:
                    par = ((k + 2) // B) % 2
                    wait(v, S["kn_done"], c + 1)
                    v.tensor_scalar(qnorm[:, k % 2, :], s.pQK[:, N:N + TILES], hp[par][:, NU_AB:NU_AB + 1],
                                    None, ALU.add).then_inc(S["qn_done"], 1)
                if head_built(k, end):
                    build_front(i, head_built(k, end))
                if head_built(k - 1, end):
                    build_back(i, head_built(k - 1, end))

            build_front(0, 0)
            build_back(0, 0)
            steps(nc.vector, a_step)
            v.wait_ge(S["acc_done"], PAIRS)
            for t in range(TT):
                last = v.bn_stats(stats[:, t, :], s.x_sb[:, t, :])
            last.then_inc(S["stat_done"], 1)
            v.wait_ge(S["stat_done"], 1)
            for t in range(TT):
                v.bn_aggr(s.mv[:, t, :], stats[:, t, :])


def program(nc, args, out):
    with ExitStack() as ctx:
        sb = lambda name, shape, dt=F32: ctx.enter_context(nc.sbuf_tensor(name, shape, dt))
        ps = lambda name, shape: ctx.enter_context(nc.psum_tensor(name, shape, F32))
        s = Shared(args, out)
        s.trig_d = nc.dram_tensor("trig_d", [3, H, DH // 2, N], F32, kind="Internal").ap()
        s.x_sb = sb("x_sb", [P, TT, D])
        s.xT = [sb(f"xT_{h}", [P, B * N], F32R) for h in ("hi", "lo")]
        s.mv = sb("mv", [P, TT, 2])
        s.w13 = [sb(f"w13_{h}", [P, 2 * HC * P], F32R) for h in ("hi", "lo")]
        s.w2s = [sb(f"w2_{h}", [P, HC * P], F32R) for h in ("hi", "lo")]
        s.wr = [sb(f"wr_{h}", [P, NE], F32R) for h in ("hi", "lo")]
        s.wp = [sb(f"wp_{h}", [P, H * P], F32R) for h in ("hi", "lo")]
        s.params = sb("params", [P, H, NPAR])
        s.ident = sb("ident", [P, P])
        s.ones = sb("ones", [P, P])
        s.dist = sb("dist", [P, SW])
        s.upper = sb("upper", [P, P])
        s.before = sb("before", [P, NE * NE])
        s.pS = ps("pS", [P, 3 * N])
        s.pQK = ps("pQK", [P, 2 * N])
        s.p5, s.p6, s.p7 = (ps(f"p{k}", [P, N]) for k in (5, 6, 7))
        setup_phase(nc, s)
        for layer in range(2):
            with (nc.sbuf_tensor(f"wT{layer}", [2 * NE, B * N], F32R) as wT,
                  nc.sbuf_tensor(f"selr{layer}", [2 * NE, HC * P], F32R) as selr):
                s.wT, s.selr = wT, selr
                norm_phase(nc, s, f"n{layer}", True)
                ffn_phase(nc, s, f"f{layer}", layer == 1)
            if layer == 0:
                norm_phase(nc, s, "na", False)
                attention_phase(nc, s)


def kernel(**inputs):
    import concourse.bacc as bacc
    from concourse.bass_utils import run_bass_kernel_spmd

    a = {k[3:]: np.asarray(v) for k, v in inputs.items()}
    c = np.ascontiguousarray

    def heads(w):
        return w.reshape(D, 2, H, DH).transpose(2, 0, 1, 3).reshape(H, D, 2 * DH)

    row, col = np.arange(P)[:, None], np.arange(N)[None, :]
    dist = np.zeros((P, SW), np.float32)
    for tile, off in OFF.items():
        w = (tile + 1) * P
        dist[:, off:off + w] = np.abs(tile * P + row - col[:, :w])
    unit = np.arange(NE * FH)[None, :] // FH
    arrays = {
        "x": c(a["attn_x"]),
        "wqk": c(np.concatenate([heads(a["attn_Wq"]), heads(a["attn_Wk"])], axis=2)),
        "wv": c(heads(a["attn_Wv"])),
        "wo": c(a["attn_Wo"].reshape(2, H, DH, D).transpose(1, 0, 2, 3).reshape(H, 2 * DH, D)),
        "omega": c(a["attn_omega"].reshape(4, P).T),
        "head_vec": c(np.stack([a["attn_" + n] for n in (
            "mu_raw", "sigma_raw", "eta_raw", "gamma_raw", "nu_raw", "tau")])),
        "w_router": c(a["ffn_w_router"].T),
        "w1": c(a["ffn_w1"]), "w3": c(a["ffn_w3"]), "w2": c(a["ffn_w2"].reshape(NE * FH, D)),
        "t_row": np.arange(N, dtype=np.float32),
        "ident_d": np.eye(P, dtype=np.float32),
        "dist_d": dist,
        "upper_d": np.where(np.arange(P)[None, :] > row, MASKED, 0.0).astype(np.float32),
        "before_d": (np.arange(NE)[None, :] < np.arange(NE)[:, None]).astype(np.float32).reshape(-1),
        "sel": c((unit == np.arange(2 * NE)[:, None] % NE).astype(np.float32)),
    }
    nc = bacc.Bacc("TRN2", target_bir_lowering=False, num_devices=1)
    args = {n: nc.dram_tensor(f"in_{n}", v.shape, F32, kind="ExternalInput").ap() for n, v in arrays.items()}
    out = nc.dram_tensor("out_x", (B, N, D), F32, kind="ExternalOutput").ap()
    program(nc, args, out)
    r = run_bass_kernel_spmd(nc, [{f"in_{n}": v for n, v in arrays.items()}], core_ids=[0])
    return r.results[0]["out_x"]
```

```python
from contextlib import ExitStack

import numpy as np
import concourse.bass as bass
from concourse import mybir

F32 = mybir.dt.float32
F32R = mybir.dt.float32r
ALU = mybir.AluOpType
ACT = mybir.ActivationFunctionType
AX = mybir.AxisListType

P = 128
D = 128
B, N = 8, 512
TILES = N // P
TT = B * TILES
H, DH = 16, 64
NE, FH = 8, 176
HC = NE * FH // P
LN_EPS = 1e-5
MU_EPS = 1e-4
MIN_EXP = -30.0
MASKED = -1e18
COEF_MIN = 1e-20
LOWEST = -3.0e38
OFF = {0: 0, 2: 128, 3: 512, 1: 1024}
ORDER = (0, 2, 3, 1)
SW = 1280
(NEG_MU, NEG_A, A_PLUS_B, LAM_SCALE, NEG_LN_NU, INV_COEF, COEF, NEG_NU_A, NU_AB, U_MIN) = range(10)
NPAR = 10
TWO_PI_HI, TWO_PI_MID = 6.28125, 0.0019350051879882812
TWO_PI_LO = float(2 * np.pi - TWO_PI_HI - TWO_PI_MID)
ROUND_MAGIC = 12582912.0
PI_BELOW = 3.1415925


def wait(eng, sem, value):
    if not (isinstance(value, int) and value <= 0):
        eng.wait_ge(sem, value)


def apart(eng, passed):
    eng.sem_inc(passed, 1)


def mm3(pe, out, lhs, rhs, start, stop):
    pe.matmul(out, lhs[1], rhs[0], start=start, stop=False)
    pe.matmul(out, lhs[0], rhs[1], start=False, stop=False)
    return pe.matmul(out, lhs[0], rhs[0], start=False, stop=stop)


class Shared:

    def __init__(self, args, out):
        self.x = args["x"]
        self.wqk = args["wqk"]
        self.wv = args["wv"]
        self.wo = args["wo"]
        self.omega = args["omega"]
        self.head_vec = args["head_vec"]
        self.w_router = args["w_router"]
        self.w1 = args["w1"]
        self.w3 = args["w3"]
        self.w2 = args["w2"]
        self.t_row = args["t_row"]
        self.ident_d = args["ident_d"]
        self.dist_d = args["dist_d"]
        self.upper_d = args["upper_d"]
        self.prio_d = args["prio_d"]
        self.sel = args["sel"]
        self.out = out


def setup_phase(nc, s):
    with ExitStack() as ctx:
        sb = lambda name, shape, dt=F32: ctx.enter_context(nc.sbuf_tensor(name, shape, dt))
        sem = lambda name: ctx.enter_context(nc.semaphore(name))
        w13_raw = sb("w13_raw", [P, 2, HC * P])
        w2_raw = sb("w2_raw", [P, HC * P])
        wr_raw = sb("wr_raw", [P, NE])
        head_in = sb("head_in", [P, 6, H])
        wv_raw = sb("wv_raw", [P, H, P])
        wo_raw = sb("wo_raw", [P, H, P])
        wvT = sb("wvT", [P, H * P])
        sc = sb("sc", [P, 16, 4 * H])

        x_in, small_in, ffn_in, cst_in = sem("x_in"), sem("small_in"), sem("ffn_in"), sem("cst_in")
        stats_raw, mv_done = sem("stats_raw"), sem("mv_done")
        hi_done, lo_done = sem("hi_done"), sem("lo_done")
        dve, act = sem("dve_chain"), sem("act_chain")
        wvo_in = sem("wvo_in")
        wv_t, wv_sb, wp_mm, wp_hi, wp_lo = (sem(n) for n in ("wv_t", "wv_sb", "wp_mm", "wp_hi", "wp_lo"))
        sm_e, sm_ln = sem("sm_e"), sem("sm_ln")
        stats = sb("stats", [P, TT, 6])
        GROUP = N // P
        turn_bank, prod_bank = (s.p6[:], s.p5[:]), (s.p7[:], s.pS[:, 0:N])

        block = ctx.enter_context(nc.Block())

        @block.sync
        def _(sp):
            x_d = s.x.rearrange("b (i p) d -> p (b i) d", p=P)
            sp.dma_start(head_in[:], s.head_vec.partition_broadcast(P)).then_inc(small_in, 16)
            sp.dma_start(s.ident[:], s.ident_d).then_inc(small_in, 16)
            for q in range(4):
                sp.dma_start(s.x_sb[:, q * 8:(q + 1) * 8, :], x_d[:, q * 8:(q + 1) * 8, :]).then_inc(x_in, 16)
            sp.dma_start(wv_raw[:], s.wv.rearrange("h d k -> d h k")).then_inc(wvo_in, 16)
            sp.dma_start(wo_raw[:], s.wo.rearrange("h d k -> d h k")).then_inc(wvo_in, 16)
            sp.dma_start(w13_raw[:, 0].rearrange("p (e h) -> p e h", e=NE),
                         s.w1.rearrange("e d h -> d e h")).then_inc(ffn_in, 16)
            sp.dma_start(w13_raw[:, 1].rearrange("p (e h) -> p e h", e=NE),
                         s.w3.rearrange("e d h -> d e h")).then_inc(ffn_in, 16)
            sp.dma_start(w2_raw[:].rearrange("p (c n) -> p c n", c=HC),
                         s.w2.rearrange("(c p) n -> p c n", p=P)).then_inc(ffn_in, 16)
            sp.dma_start(wr_raw[:], s.w_router).then_inc(ffn_in, 16)
            sp.dma_start(s.dist[:], s.dist_d).then_inc(cst_in, 16)
            sp.dma_start(s.upper[:], s.upper_d).then_inc(cst_in, 16)
            sp.dma_start(s.prio[:], s.prio_d.partition_broadcast(P)).then_inc(cst_in, 16)
            sp.wait_ge(cst_in, 48)

        @block.tensor
        def _(pe):
            pe.wait_ge(small_in, 32)
            pe.wait_ge(wvo_in, 32)
            for g in range(H // GROUP):
                if g >= 2:
                    pe.wait_ge(wv_sb, g - 1)
                for k in range(GROUP):
                    last = pe.transpose(turn_bank[g % 2][:, k * P:(k + 1) * P], wv_raw[:, g * GROUP + k], s.ident[:])
                last.then_inc(wv_t, 1)
                pe.wait_ge(wv_sb, g + 1)
                if g >= 2:
                    pe.wait_ge(wp_lo, g - 1)
                for k in range(GROUP):
                    h = g * GROUP + k
                    last = pe.matmul(prod_bank[g % 2][:, k * P:(k + 1) * P], wvT[:, h * P:(h + 1) * P],
                                     wo_raw[:, h], start=True, stop=True)
                last.then_inc(wp_mm, 1)

        @block.scalar
        def _(a):
            nc.scalar.preload_act_table_set("natural_log_exp_and_others")
            a.wait_ge(sm_e, 1)
            a.activation(sc[:, 0, 0:H], head_in[:, 0], ACT.Exp, scale=-1.0).then_inc(sm_ln, 1)
            a.activation(sc[:, 2], sc[:, 1], ACT.Exp, scale=-1.0).then_inc(sm_ln, 1)
            a.wait_ge(sm_e, 2)
            a.activation(sc[:, 4], sc[:, 3], ACT.Ln).then_inc(sm_ln, 1)
            a.wait_ge(sm_e, 3)
            a.activation(sc[:, 10, 0:H], sc[:, 8, 3 * H:4 * H], ACT.Ln).then_inc(sm_ln, 1)
            for g in range(H // GROUP):
                cols = slice(g * N, (g + 1) * N)
                a.wait_ge(wv_t, g + 1)
                a.activation(wvT[:, cols], turn_bank[g % 2], ACT.Copy).then_inc(wv_sb, 1)
                a.wait_ge(wp_mm, g + 1)
                a.activation(s.wp[0][:, cols], prod_bank[g % 2], ACT.Copy).then_inc(wp_hi, 1)
            a.wait_ge(ffn_in, 64)
            a.activation(s.w2s[0][:], w2_raw[:], ACT.Copy).then_inc(hi_done, 1)
            for k in range(2):
                a.activation(s.w13[0][:, k * HC * P:(k + 1) * HC * P], w13_raw[:, k], ACT.Copy).then_inc(hi_done, 1)
            a.activation(s.wr[0][:], wr_raw[:], ACT.Copy).then_inc(hi_done, 1)

        @block.vector
        def _(v):
            count = [0]

            def step(ins):
                count[0] += 1
                ins.then_inc(dve, 1)
                v.wait_ge(dve, count[0])

            v.memset(s.ones[:], 1.0)
            v.wait_ge(small_in, 32)
            raw = head_in[:, 1:5].rearrange("p a h -> p (a h)")
            q = lambda k, j: sc[:, k, j * H:(j + 1) * H]
            ts, tt, stt = v.tensor_scalar, v.tensor_tensor, v.scalar_tensor_tensor
            step(ts(sc[:, 5], raw, -1.0, None, ALU.mult))
            step(tt(sc[:, 1], sc[:, 5], raw, ALU.max))
            v.memset(sc[:, 12], 0.0).then_inc(sm_e, 1)
            v.wait_ge(sm_ln, 2)
            step(ts(sc[:, 3], sc[:, 2], 1.0, None, ALU.add))
            v.memset(sc[:, 13], 0.0).then_inc(sm_e, 1)
            step(ts(sc[:, 5], sc[:, 3], -1.0, None, ALU.add))
            step(ts(sc[:, 6], sc[:, 5], 0.0, None, ALU.is_equal))
            step(tt(sc[:, 5], sc[:, 5], sc[:, 6], ALU.add))
            step(v.reciprocal(sc[:, 7], sc[:, 5]))
            step(tt(sc[:, 7], sc[:, 7], sc[:, 2], ALU.mult))
            v.wait_ge(sm_ln, 3)
            step(tt(sc[:, 7], sc[:, 7], sc[:, 4], ALU.mult))
            step(tt(sc[:, 6], sc[:, 6], sc[:, 2], ALU.mult))
            step(tt(sc[:, 7], sc[:, 7], sc[:, 6], ALU.add))
            step(stt(sc[:, 8], raw, 0.0, sc[:, 7], ALU.max, ALU.add))
            v.memset(sc[:, 14], 0.0).then_inc(sm_e, 1)
            sigma, eta, gamma, nu = (q(8, j) for j in range(4))
            par = lambda k: s.params[:, :, k]
            step(ts(q(9, 0), sc[:, 0, 0:H], 1.0, None, ALU.add))
            step(v.reciprocal(q(9, 1), q(9, 0)))
            step(ts(q(9, 2), q(9, 1), MU_EPS, None, ALU.add))
            step(ts(par(NEG_MU), q(9, 2), -1.0, None, ALU.mult))
            step(v.reciprocal(q(9, 3), q(9, 2)))
            step(tt(q(9, 3), q(9, 3), sigma, ALU.mult))
            step(ts(q(9, 3), q(9, 3), 0.5, None, ALU.mult))
            step(ts(par(NEG_A), q(9, 3), -1.0, None, ALU.mult))
            step(tt(q(11, 0), eta, gamma, ALU.add))
            step(tt(par(A_PLUS_B), q(11, 0), q(9, 3), ALU.add))
            step(tt(par(NEG_NU_A), par(NEG_A), nu, ALU.mult))
            step(tt(par(NU_AB), par(A_PLUS_B), nu, ALU.mult))
            step(tt(par(U_MIN), q(11, 0), nu, ALU.mult))
            step(ts(q(11, 1), nu, float(DH), -0.5, ALU.add, ALU.mult))
            step(tt(q(11, 1), q(11, 1), head_in[:, 5], ALU.mult))
            step(ts(q(11, 2), q(11, 1), -1.0, None, ALU.mult))
            step(tt(q(11, 2), q(11, 2), q(11, 1), ALU.max))
            step(ts(q(11, 2), q(11, 2), COEF_MIN, -COEF_MIN, ALU.is_lt, ALU.mult))
            step(ts(q(11, 3), q(11, 2), 1.0 / COEF_MIN, 1.0, ALU.mult, ALU.add))
            step(tt(q(11, 1), q(11, 1), q(11, 3), ALU.mult))
            step(tt(par(COEF), q(11, 1), q(11, 2), ALU.add))
            step(v.reciprocal(par(INV_COEF), par(COEF)))
            step(ts(par(LAM_SCALE), par(INV_COEF), -0.5 * DH, -1.0, ALU.mult, ALU.add))
            v.wait_ge(sm_ln, 4)
            step(ts(par(NEG_LN_NU), sc[:, 10, 0:H], -1.0, None, ALU.mult))

            v.wait_ge(x_in, 64)
            for t in range(TT):
                last = v.bn_stats(stats[:, t, :], s.x_sb[:, t, :])
            last.then_inc(stats_raw, 1)
            v.wait_ge(stats_raw, 1)
            for t in range(TT):
                v.bn_aggr(s.mv[:, t, :], stats[:, t, :]).then_inc(mv_done, 1)
            for g in range(H // GROUP):
                cols = slice(g * N, (g + 1) * N)
                v.wait_ge(wp_hi, g + 1)
                v.tensor_tensor(s.wp[1][:, cols], prod_bank[g % 2], s.wp[0][:, cols].bitcast(F32),
                                ALU.subtract).then_inc(wp_lo, 1)
            for k in range(2):
                cols = slice(k * HC * P, (k + 1) * HC * P)
                v.wait_ge(hi_done, k + 2)
                v.tensor_tensor(s.w13[1][:, cols], w13_raw[:, k], s.w13[0][:, cols].bitcast(F32),
                                ALU.subtract).then_inc(lo_done, 1)
            v.wait_ge(hi_done, 4)
            v.tensor_tensor(s.wr[1][:], wr_raw[:], s.wr[0][:].bitcast(F32), ALU.subtract).then_inc(lo_done, 1)

        @block.gpsimd
        def _(g):
            g.wait_ge(hi_done, 1)
            g.tensor_tensor(s.w2s[1][:], w2_raw[:], s.w2s[0][:].bitcast(F32), ALU.subtract).then_inc(lo_done, 1)


def norm_phase(nc, s, tag, route):
    with ExitStack() as ctx:
        sb = lambda name, shape, dt=F32: ctx.enter_context(nc.sbuf_tensor(f"{name}_{tag}", shape, dt))
        sem = lambda name: ctx.enter_context(nc.semaphore(f"{name}_{tag}"))
        var = sb("var", [P, TT])
        root = sb("root", [P, TT])
        rstd = sb("rstd", [P, TT])
        tmp = sb("tmp", [P, TT])
        shift = sb("shift", [P, TT])
        DEEP = 4
        xn = sb("xn", [P, DEEP, TILES, P])
        dve, root_done = sem("dve_chain"), sem("root_done")
        shift_done, xn_act = sem("shift_done"), sem("xn_act")
        BY_DVE = TILES // 2
        var_done, xn_done, xt_done, xhi_done, xlo_done = (sem(n) for n in (
            "var_done", "xn_done", "xt_done", "xhi_done", "xlo_done"))
        score_in, exp_done, w_done, wt_done = (sem(n) for n in ("score_in", "exp_done", "w_done", "wt_done"))
        wt_copied = (sem("wt_copied_act"), sem("wt_copied_dve"))
        if route:
            e_s = sb("e_s", [P, TT, NE])
            sm = sb("sm", [P, 3, TT])
            logitT = sb("logitT", [NE, 2, N])
            pick = sb("pick", [P, 2, TT, NE])
            rest = sb("rest", [P, TT, NE])
            hi_r = sb("hi_r", [P, TT, NE], F32R)
            w16 = sb("w16", [P, TT, 2 * NE])
            sel_raw = sb("sel_raw", [2 * NE, HC * P])
            sel_in, sel_done = sem("sel_in"), sem("sel_done")
            product_done, product_sb, turned = sem("product_done"), sem("product_sb"), sem("turned")
        banks = (s.pS[:, 0:N], s.pS[:, N:2 * N], s.pQK[:, 0:N], s.pQK[:, N:2 * N])
        product_bank = (s.p5[0:NE, :], s.p6[0:NE, :])
        weight_bank = (s.pS[0:2 * NE, 0:N], s.pS[0:2 * NE, N:2 * N], s.p5[0:2 * NE, :], s.p6[0:2 * NE, :])
        logits = s.p7[:, 0:TT * NE].rearrange("p (t e) -> p t e", e=NE)
        flat = lambda t: t.rearrange("p a b -> p (a b)")
        block = ctx.enter_context(nc.Block())

        if route:
            @block.sync
            def _(sp):
                sp.dma_start(sel_raw[:], s.sel).then_inc(sel_in, 16)

        @block.tensor
        def _(pe):
            def turn(i, k):
                pe.wait_ge(xn_done, i * DEEP + k + 1)
                pe.wait_ge(xn_act, i * DEEP + k + 1)
                wait(pe, xlo_done, i * DEEP)
                for q in range(TILES):
                    last = pe.transpose(banks[k][:, q * P:(q + 1) * P], xn[:, k, q], s.ident[:])
                last.then_inc(xt_done, 1)

            def product(c):
                toks = slice(c * N, (c + 1) * N)
                pe.wait_ge(xlo_done, c + 1)
                wait(pe, product_sb, c - 1)
                mm3(pe, product_bank[c % 2], (s.wr[0][:], s.wr[1][:]), (s.xT[0][:, toks], s.xT[1][:, toks]),
                    True, True).then_inc(product_done, 1)

            def turn_product(c):
                pe.wait_ge(product_sb, c + 1)
                for k in range(TILES):
                    last = pe.transpose(logits[:, c * TILES + k], logitT[:, c % 2, k * P:(k + 1) * P],
                                        s.ident[0:NE, 0:NE])
                last.then_inc(turned, 1)

            if not route:
                with nc.tensor.Fori(0, B // DEEP) as i:
                    for k in range(DEEP):
                        turn(i, k)
            else:
                for c in range(B + DEEP):
                    if c < B:
                        turn(c // DEEP, c % DEEP)
                    if DEEP - 1 <= c < B + DEEP - 1:
                        product(c - DEEP + 1)
                    if c >= DEEP:
                        turn_product(c - DEEP)
                pe.wait_ge(w_done, 1)
                for c in range(B):
                    if c >= 4:
                        pe.wait_ge(wt_copied[c % 2], c // 2 - 1)
                    for k in range(TILES):
                        last = pe.transpose(weight_bank[c % 4][:, k * P:(k + 1) * P],
                                            w16[:, c * TILES + k, :], s.ident[:])
                    last.then_inc(wt_done, 1)

        @block.scalar
        def _(a):
            a.wait_ge(var_done, 1)
            a.activation(root[:], var[:], ACT.Sqrt).then_inc(root_done, 1)
            nc.scalar.preload_act_table_set("natural_log_exp_and_others")
            def normalise(i, k):
                for q in range(BY_DVE, TILES):
                    t = (i * DEEP + k) * TILES + q
                    last = a.activation(xn[:, k, q], s.x_sb[:, bass.ds(t, 1), :].rearrange("p a d -> p (a d)"),
                                        ACT.Identity, bias=shift[:, bass.ds(t, 1)], scale=rstd[:, bass.ds(t, 1)])
                last.then_inc(xn_act, 1)

            def high(i, k):
                a.wait_ge(xt_done, i * DEEP + k + 1)
                a.activation(s.xT[0][:, bass.ds((i * DEEP + k) * N, N)], banks[k], ACT.Copy).then_inc(xhi_done, 1)

            a.wait_ge(shift_done, 1)
            if not route:
                with nc.scalar.Fori(0, B // DEEP) as i:
                    a.wait_ge(xt_done, i * DEEP)
                    for k in range(DEEP):
                        normalise(i, k)
                    for k in range(DEEP):
                        high(i, k)
            else:
                a.wait_ge(sel_in, 16)
                a.activation(s.selr[:], sel_raw[:], ACT.Copy).then_inc(sel_done, 1)
                for c in range(B + DEEP - 1):
                    if c < B and c % DEEP == 0:
                        wait(a, xt_done, c)
                        for k in range(DEEP):
                            normalise(c // DEEP, k)
                    if c < B:
                        high(c // DEEP, c % DEEP)
                    if c >= DEEP - 1:
                        q = c - DEEP + 1
                        a.wait_ge(product_done, q + 1)
                        wait(a, turned, q - 1)
                        a.activation(logitT[:, q % 2], product_bank[q % 2], ACT.Copy).then_inc(product_sb, 1)
                a.wait_ge(score_in, 1)
                a.activation(e_s[:], e_s[:], ACT.Exp).then_inc(exp_done, 1)
                for c in range(0, B, 2):
                    a.wait_ge(wt_done, c + 1)
                    a.activation(s.wT[:, c * N:(c + 1) * N], weight_bank[c % 4], ACT.Copy).then_inc(wt_copied[0], 1)

        @block.vector
        def _(v):
            count = [0]

            def step(ins):
                count[0] += 1
                ins.then_inc(dve, 1)
                v.wait_ge(dve, count[0])

            v.tensor_scalar(var[:], s.mv[:, :, 1], LN_EPS, None, ALU.add).then_inc(var_done, 1)
            v.wait_ge(root_done, 1)
            step(v.reciprocal(rstd[:], root[:]))
            step(v.tensor_tensor(tmp[:], rstd[:], rstd[:], ALU.mult))
            step(v.tensor_tensor(tmp[:], tmp[:], var[:], ALU.mult))
            step(v.tensor_scalar(tmp[:], tmp[:], -0.5, 1.5, ALU.mult, ALU.add))
            step(v.tensor_tensor(rstd[:], rstd[:], tmp[:], ALU.mult))
            v.scalar_tensor_tensor(shift[:], s.mv[:, :, 0], -1.0, rstd[:], ALU.mult, ALU.mult).then_inc(shift_done, 1)

            def normalise(i, k):
                for q in range(BY_DVE):
                    t = (i * DEEP + k) * TILES + q
                    last = v.tensor_scalar(xn[:, k, q], s.x_sb[:, bass.ds(t, 1), :].rearrange("p a d -> p (a d)"),
                                           s.mv[:, bass.ds(t, 1), 0], rstd[:, bass.ds(t, 1)],
                                           ALU.subtract, ALU.mult)
                last.then_inc(xn_done, 1)

            def low(i, k):
                v.wait_ge(xhi_done, i * DEEP + k + 1)
                cols = bass.ds((i * DEEP + k) * N, N)
                v.tensor_tensor(s.xT[1][:, cols], banks[k], s.xT[0][:, cols].bitcast(F32),
                                ALU.subtract).then_inc(xlo_done, 1)

            with nc.vector.Fori(0, B // DEEP) as i:
                v.wait_ge(xt_done, i * DEEP)
                for k in range(DEEP):
                    normalise(i, k)
                for k in range(DEEP):
                    low(i, k)
            if route:
                v.wait_ge(turned, B)
                wide = lambda t: t.unsqueeze(2).broadcast_to([P, TT, NE])
                step(v.tensor_reduce(sm[:, 0], logits, AX.X, ALU.max))
                v.tensor_tensor(e_s[:], logits, wide(sm[:, 0]), ALU.subtract).then_inc(score_in, 1)
                v.wait_ge(exp_done, 1)
                step(v.tensor_reduce(sm[:, 1], e_s[:], AX.X, ALU.add))
                step(v.reciprocal(sm[:, 2], sm[:, 1]))
                step(v.tensor_tensor(e_s[:], e_s[:], wide(sm[:, 2]), ALU.mult))
                prio = s.prio[:].unsqueeze(1).broadcast_to([P, TT, NE])
                for k, src in enumerate((e_s, rest)):
                    step(v.tensor_reduce(sm[:, 0], src[:], AX.X, ALU.max))
                    step(v.tensor_tensor(pick[:, k], src[:], wide(sm[:, 0]), ALU.is_equal))
                    step(v.tensor_tensor(pick[:, k], pick[:, k], prio, ALU.mult))
                    step(v.tensor_reduce(sm[:, 1], pick[:, k], AX.X, ALU.max))
                    step(v.tensor_tensor(pick[:, k], pick[:, k], wide(sm[:, 1]), ALU.is_equal))
                    if k == 0:
                        step(v.scalar_tensor_tensor(flat(rest[:]), flat(pick[:, 0]), -2.0, flat(e_s[:]),
                                                    ALU.mult, ALU.add))
                step(v.tensor_tensor(pick[:, 0], pick[:, 0], pick[:, 1], ALU.add))
                step(v.tensor_tensor(e_s[:], e_s[:], pick[:, 0], ALU.mult))
                step(v.tensor_copy(hi_r[:], e_s[:]))
                step(v.tensor_copy(w16[:, :, 0:NE], hi_r[:].bitcast(F32)))
                v.tensor_tensor(w16[:, :, NE:2 * NE], e_s[:], hi_r[:].bitcast(F32),
                                ALU.subtract).then_inc(w_done, 1)
                for c in range(1, B, 2):
                    v.wait_ge(wt_done, c + 1)
                    v.tensor_copy(s.wT[:, c * N:(c + 1) * N], weight_bank[c % 4]).then_inc(wt_copied[1], 1)


def ffn_phase(nc, s, tag, last_phase, rotary):
    with ExitStack() as ctx:
        sb = lambda name, shape, dt=F32: ctx.enter_context(nc.sbuf_tensor(f"{name}_{tag}", shape, dt))
        sem = lambda name: ctx.enter_context(nc.semaphore(f"{name}_{tag}"))
        silu = sb("silu", [P, 2, N])
        gated = sb("gated", [P, 2, N])
        hid = sb("hid", [P, 2, N])
        hid_hi = sb("hid_hi", [P, 2, N], F32R)
        hid_lo = sb("hid_lo", [P, 2, N], F32R)
        yT = sb("yT", [P, N])
        stats = sb("stats", [P, TILES, 6])
        mean_var = sb("mean_var", [P, TILES, 2])
        aggr_done, pe_passed, dve_passed = sem("aggr_done"), sem("pe_passed"), sem("dve_passed")
        guw_done, silu_done, gated_done, hid_done, hi_done, lo_done = (sem(n) for n in (
            "guw_done", "silu_done", "gated_done", "hid_done", "hi_done", "lo_done"))
        y_slot, y_out, y_turned, x_done, stat_done, stored = (sem(n) for n in (
            "y_slot", "y_out", "y_turned", "x_done", "stat_done", "stored"))
        g_bank = (s.pS[:, 0:N], s.pQK[:, 0:N])
        u_bank = (s.pS[:, N:2 * N], s.pQK[:, N:2 * N])
        w_bank = (s.pS[:, 2 * N:3 * N], s.p5[:])
        y_bank = (s.p6[:], s.p7[:])
        SLOTS = 2 * HC
        COPY, TURN, ADD, STATS, AGGR, KEEP, AHEAD = range(7)
        if rotary:
            omega = sb("omega", [P, 4])
            t_row = sb("t_row", [P, N])
            ang = sb("ang", [P, 4, N])
            turns = sb("turns", [P, 2, 4, N])
            reduced = sb("reduced", [P, 2, 4, N])
            pool, angle_in, angles, trig_done, trig_neg, trig_out = (sem(n) for n in (
                "pool_chain", "angle_in", "angles", "trig_done", "trig_neg", "trig_out"))
        block = ctx.enter_context(nc.Block())

        def slots(eng, body):
            for u in range(AHEAD):
                body(0, u, False, False)
            with eng.Fori(0, B // 2 - 1) as i:
                for u in range(AHEAD, SLOTS + AHEAD):
                    body(i, u, False, u >= HC)
            for u in range(AHEAD, SLOTS):
                body(B // 2 - 1, u, True, u >= HC)

        @block.tensor
        def _(pe):
            def products(i, u):
                e, k, c, par = i * SLOTS + u, u % HC, i * 2 + u // HC, u % 2
                hid_cols = slice(k * P, (k + 1) * P)
                up_cols = slice((HC + k) * P, (HC + k + 1) * P)
                toks = bass.ds(c * N, N)
                xT = (s.xT[0][:, toks], s.xT[1][:, toks])
                wait(pe, silu_done, e - 1)
                mm3(pe, g_bank[par], tuple(w[:, hid_cols] for w in s.w13), xT, True, True)
                wait(pe, gated_done, e - 1)
                mm3(pe, u_bank[par], tuple(w[:, up_cols] for w in s.w13), xT, True, True)
                wait(pe, hid_done, e - 1)
                apart(pe, pe_passed)
                pe.matmul(w_bank[par], s.selr[:, hid_cols], s.wT[:, toks],
                          start=True, stop=True).then_inc(guw_done, 1)

            products(0, 0)
            products(0, 1)

            def turn(c, par):
                pe.wait_ge(y_out, c + 1)
                for k in range(TILES):
                    last = pe.transpose(y_bank[par][:, k * P:(k + 1) * P], yT[:, k * P:(k + 1) * P], s.ident[:])
                last.then_inc(y_turned, 1)

            def body(i, u, end, before):
                e, k, c, par = i * SLOTS + u, u % HC, i * 2 + u // HC, u % 2
                if not (end and u + 2 >= SLOTS):
                    products(i, u + 2)
                pe.wait_ge(lo_done, e + 1)
                if k == 0:
                    wait(pe, x_done, c - 1)
                mm3(pe, y_bank[(u // HC) % 2], tuple(w[:, k * P:(k + 1) * P] for w in s.w2s),
                    (hid_hi[:, par], hid_lo[:, par]), k == 0, k == HC - 1).then_inc(y_slot, 1)
                if before and k == TURN:
                    turn(c - 1, (u // HC - 1) % 2)

            slots(nc.tensor, body)
            turn(B - 1, 1)

        @block.scalar
        def _(a):
            def do_silu(i, u):
                e, par = i * SLOTS + u, u % 2
                a.wait_ge(guw_done, e + 1)
                wait(a, gated_done, e - 1)
                a.activation(silu[:, par], g_bank[par], ACT.Silu).then_inc(silu_done, 1)

            def copy_out(c, par):
                a.wait_ge(y_slot, (c + 1) * HC)
                wait(a, y_turned, c)
                a.activation(yT[:], y_bank[par], ACT.Copy, scale=0.5).then_inc(y_out, 1)

            def body(i, u, end, before):
                e, k, c, par = i * SLOTS + u, u % HC, i * 2 + u // HC, u % 2
                if not (end and u + 1 == SLOTS):
                    do_silu(i, u + 1)
                a.wait_ge(hid_done, e + 1)
                wait(a, y_slot, e - 1)
                a.activation(hid_hi[:, par], hid[:, par], ACT.Copy).then_inc(hi_done, 1)
                if before and k == COPY:
                    copy_out(c - 1, (u // HC - 1) % 2)
                if rotary and end and u == AHEAD:
                    a.wait_ge(angles, 1)
                    a.activation(reduced[:, 1], reduced[:, 1], ACT.Sin).then_inc(trig_done, 1)
                    a.activation(turns[:, 0], reduced[:, 0], ACT.Sin).then_inc(trig_done, 1)

            do_silu(0, 0)
            slots(nc.scalar, body)
            copy_out(B - 1, 1)

        @block.vector
        def _(v):
            def gate(i, u):
                e, par = i * SLOTS + u, u % 2
                v.wait_ge(silu_done, e + 1)
                v.tensor_tensor(gated[:, par], u_bank[par], silu[:, par], ALU.mult).then_inc(gated_done, 1)

            def body(i, u, end, before):
                e, k, c, par = i * SLOTS + u, u % HC, i * 2 + u // HC, u % 2
                v.wait_ge(gated_done, e + 1)
                v.tensor_tensor(hid[:, par], w_bank[par], gated[:, par], ALU.mult).then_inc(hid_done, 1)
                if not (end and u + 1 == SLOTS):
                    gate(i, u + 1)
                v.wait_ge(hi_done, e + 1)
                wait(v, y_slot, e - 1)
                v.tensor_tensor(hid_lo[:, par], hid[:, par], hid_hi[:, par].bitcast(F32),
                                ALU.subtract).then_inc(lo_done, 1)
                if before and ADD <= k <= KEEP:
                    finish(c - 1, (u // HC - 1) % 2, k)

            def finish(c, par, part):
                if part == ADD:
                    v.wait_ge(y_turned, c + 1)
                    xc = s.x_sb[:, bass.ds(c * TILES, TILES), :]
                    v.tensor_tensor(xc, y_bank[par].rearrange("p (a b) -> p a b", a=TILES), xc,
                                    ALU.add).then_inc(x_done, 1)
                elif last_phase:
                    return
                elif part == STATS:
                    v.wait_ge(x_done, c + 1)
                    apart(v, dve_passed)
                    for k in range(TILES):
                        last = v.bn_stats(stats[:, k, :],
                                          s.x_sb[:, bass.ds(c * TILES + k, 1), :].rearrange("p a d -> p (a d)"))
                    last.then_inc(stat_done, 1)
                elif part == AGGR:
                    v.wait_ge(stat_done, c + 1)
                    apart(v, dve_passed)
                    for k in range(TILES):
                        last = v.bn_aggr(mean_var[:, k, :], stats[:, k, :])
                    last.then_inc(aggr_done, 1)
                elif part == KEEP:
                    v.wait_ge(aggr_done, c + 1)
                    v.tensor_copy(s.mv[:, bass.ds(c * TILES, TILES), :], mean_var[:])

            gate(0, 0)
            slots(nc.vector, body)
            for part in (ADD, STATS, AGGR, KEEP):
                finish(B - 1, 1, part)

        if rotary:
            @block.gpsimd
            def _(g):
                count = [0]

                def step(ins):
                    count[0] += 1
                    ins.then_inc(pool, 1)
                    g.wait_ge(pool, count[0])

                g.wait_ge(angle_in, 32)
                for k in range(4):
                    last = g.tensor_scalar(ang[:, k], t_row[:], omega[:, k:k + 1], None, ALU.mult)
                step(last)
                for k, quarter in enumerate((0.0, 0.25)):
                    step(g.tensor_scalar(turns[:, k], ang[:], float(1 / (2 * np.pi)), quarter, ALU.mult, ALU.add))
                    step(g.tensor_scalar(turns[:, k], turns[:, k], ROUND_MAGIC, ROUND_MAGIC, ALU.add, ALU.subtract))
                    src = ang[:]
                    whole = reduced[:, 1] if k == 0 else turns[:, 0]
                    for part in (TWO_PI_HI, TWO_PI_MID, TWO_PI_LO):
                        step(g.tensor_scalar(whole, turns[:, k], -part, None, ALU.mult))
                        step(g.tensor_tensor(reduced[:, k], src, whole, ALU.add))
                        src = reduced[:, k]
                    step(g.tensor_scalar(reduced[:, k], reduced[:, k], float(np.pi / 2) * k, PI_BELOW,
                                         ALU.add, ALU.min))
                    last = g.tensor_scalar(reduced[:, k], reduced[:, k], -PI_BELOW, None, ALU.max)
                    if k == 0:
                        step(last)
                last.then_inc(angles, 1)
                g.wait_ge(trig_done, 2)
                g.tensor_scalar(turns[:, 1], turns[:, 0], -1.0, None, ALU.mult).then_inc(trig_neg, 1)

            @block.sync
            def _(sp):
                sp.dma_start(omega[:], s.omega).then_inc(angle_in, 16)
                sp.dma_start(t_row[:], s.t_row.partition_broadcast(P)).then_inc(angle_in, 16)
                sp.wait_ge(trig_done, 2)
                sp.wait_ge(trig_neg, 1)
                for k, table in enumerate((reduced[:, 1], turns[:, 0], turns[:, 1])):
                    sp.dma_start(s.trig_d[k].rearrange("(g q) d t -> (q d) g t", q=4), table).then_inc(trig_out, 16)
                sp.wait_ge(trig_out, 48)

        if last_phase:
            @block.sync
            def _(sp):
                for c in range(B):
                    sp.wait_ge(x_done, c + 1)
                    sp.dma_start(s.out.rearrange("b (i p) d -> p b i d", p=P)[:, c],
                                 s.x_sb[:, c * TILES:(c + 1) * TILES, :]).then_inc(stored, 16)
                sp.wait_ge(stored, 16 * B)


def attention_phase(nc, s):
    PAIRS = H * B
    with ExitStack() as ctx:
        sb = lambda name, shape, dt=F32: ctx.enter_context(nc.sbuf_tensor(name, shape, dt))
        sem = lambda name: ctx.enter_context(nc.semaphore(name))
        decay = [sb(f"decay{k}", [P, SW]) for k in range(2)]
        decay2 = [sb(f"decay2_{k}", [P, SW]) for k in range(2)]
        lam = [sb(f"lam{k}", [P, SW]) for k in range(2)]
        cos = [sb(f"cos{k}", [P, N]) for k in range(2)]
        sin = [sb(f"sin{k}", [P, N]) for k in range(2)]
        hp = [sb(f"hp{k}", [P, NPAR]) for k in range(2)]
        wqk_raw = sb("wqk_raw", [P, 2 * P])
        wqk = [[sb(f"wqk_{half}{k}", [P, 2 * P], F32R) for half in ("hi", "lo")] for k in range(2)]
        swapped = sb("swapped", [P, 2 * N])
        by_cos = sb("by_cos", [P, 2 * N])
        squares = sb("squares", [P, 2 * N])
        rot = sb("rot", [P, 2 * N])
        knorm = sb("knorm", [P, N])
        qnorm = sb("qnorm", [P, 2, TILES])
        ek = sb("ek", [P, SW])
        u = sb("u", [P, SW])
        z = sb("z", [P, SW])
        probT = sb("probT", [P, SW])
        val_even = [sb(f"val_even{k}", [P, N]) for k in range(2)]
        val_odd = [sb(f"val_odd{b}", [P, N]) for b in range(B)]
        zmax = sb("zmax", [P, TILES])
        nmax = sb("nmax", [P, TILES])
        rsum = sb("rsum", [P, 2, TILES])
        rinv = sb("rinv", [P, 2, TILES])
        stats = sb("stats_at", [P, TT, 6])
        names = ("w_in trig_in0 trig_in1 w_hi w_lo hp_done arg_done decay_done decay2_done lnv_done lam0_done "
                 "lam_done qk_done swap_done cos_done sin_done sq_done rot_done norm_done q2_done qn_done kn_done "
                 "ek_done s_done es_done sum_done u_done ln_done zred_done nmax_done exp_done v_done "
                 "val_done tr_done trc_done av_done rinv_done acc_done stat_done dve_passed pool_passed")
        S = {n: sem(n) for n in names.split()}
        trig_in = (S["trig_in0"], S["trig_in1"])
        block = ctx.enter_context(nc.Block())

        both = lambda t: t[:].unsqueeze(1).broadcast_to([P, 2, N])
        two = lambda t: t.rearrange("p (a t) -> p a t", a=2)

        def steps(eng, a_step):
            for k in (-3, -2, -1):
                a_step(0, k, False)
            with eng.Fori(0, H // 2 - 1) as i:
                for k in range(16):
                    a_step(i, k, False)
            for k in range(16):
                a_step(H // 2 - 1, k, True)

        def stages(k, end):
            return (k >= 0 and not (end and k >= 16), -1 <= k and not (end and k + 1 >= 16),
                    -2 <= k and not (end and k + 2 >= 16))

        def makes_values(k):
            return ((k + 1) // B) % 2 == 0

        def norms_late(k):
            return not makes_values(k)

        def norms_by_vector(k):
            return k in (EXP, SQUARE, LN)

        def values_made(i, k):
            return i * B + min(k + 1, B)

        FRONT, EXP, SQUARE, LN, LAM, MASK = range(2, 8)

        def building(part, k, end):
            if k == part:
                return 1
            if k == part + B and not end:
                return 2
            return None

        @block.sync
        def _(sp):
            def load(i, off):
                h, par = i * 2 + off, off % 2
                wait(sp, S["w_lo"], h)
                sp.dma_start(wqk_raw[:], s.wqk[h]).then_inc(S["w_in"], 16)
                wait(sp, S["sin_done"], (i * 2 + off - 1) * B)
                wait(sp, S["cos_done"], (i * 2 + off - 1) * B)
                for g in range(4):
                    rows = slice(32 * g, 32 * g + 32)
                    sp.dma_start(cos[par][rows, :], s.trig_d[0, h]).then_inc(trig_in[par], 16)
                    which = (2, 1, 1, 2)[g]
                    sp.dma_start(sin[par][rows, :], s.trig_d[which, h]).then_inc(trig_in[par], 16)

            load(0, 0)
            with nc.sync.Fori(0, H // 2 - 1) as i:
                load(i, 1)
                load(i, 2)
            load(H // 2 - 1, 1)

        @block.tensor
        def _(pe):
            def a_step(i, k, end):
                n = i * 16 + k
                out, score, proj = stages(k, end)
                m, c = n + 1, n + 2
                def project(j):
                    if k >= -3 and not (end and k + 3 >= 16):
                        q, par, b = n + 3, ((k + 3) // B) % 2, (k + 3) % B
                        head = i * 2 + (k + 3) // B
                        if j == 0:
                            wait(pe, S["w_hi"], head + 1)
                            wait(pe, S["w_lo"], head + 1)
                            wait(pe, S["swap_done"], q)
                        toks = slice(b * N, (b + 1) * N)
                        last = mm3(pe, s.pQK[:, j * N:(j + 1) * N], tuple(w[:, j * P:(j + 1) * P] for w in wqk[par]),
                                   (s.xT[0][:, toks], s.xT[1][:, toks]), True, True)
                        if j == 1:
                            last.then_inc(S["qk_done"], 1)

                def query_norms():
                    wait(pe, S["sq_done"], c + 1)
                    if out:
                        wait(pe, S["val_done"], values_made(i, k))
                    wait(pe, S["qn_done"], c)
                    for I in range(TILES):
                        last = pe.matmul(s.p5[:, I:I + 1], squares[:, I * P:(I + 1) * P],
                                         s.ones[:, 0:1], start=True, stop=True)
                    last.then_inc(S["q2_done"], 1)

                def key_norms():
                    wait(pe, S["norm_done"], c)
                    pe.matmul(s.p6[:], s.ones[:], squares[:, N:2 * N], start=True, stop=True).then_inc(S["kn_done"], 1)

                project(0)
                if norms_late(k):
                    project(1)
                if proj and not norms_late(k):
                    query_norms()
                    key_norms()
                if out:
                    wait(pe, S["exp_done"], n + 1)
                    wait(pe, S["es_done"], min(n + 2, PAIRS) if end else n + 2)
                    for col in range(0, SW, P):
                        last = pe.transpose(s.pS[:, col:col + P], z[:, col:col + P], s.ident[:])
                    last.then_inc(S["tr_done"], 1)
                if proj and norms_late(k):
                    query_norms()
                    key_norms()
                if not norms_late(k):
                    project(1)
                if score and makes_values(k):
                    b = (k + 1) % B
                    wait(pe, S["qn_done"], c + 1)
                    wo = tuple(w[:, bass.ds((i * 2 + (k + 1) // B) * P, 2 * P)] for w in s.wp)
                    for J in range(TILES):
                        if J == TILES // 2:
                            wait(pe, S["norm_done"], c + 1)
                        t = slice((b * TILES + J) * P, (b * TILES + J + 1) * P)
                        last = mm3(pe, s.pV[:, 2 * J * P:2 * (J + 1) * P], (s.xT[0][:, t], s.xT[1][:, t]), wo, True, True)
                    last.then_inc(S["v_done"], 1)
                if proj:
                    wait(pe, S["rot_done"], c + 1)
                    if out:
                        wait(pe, S["trc_done"], n + 1)
                    else:
                        wait(pe, S["es_done"], c)
                    for I in ORDER:
                        last = pe.matmul(s.pS[:, OFF[I]:OFF[I] + (I + 1) * P], rot[:, I * P:(I + 1) * P],
                                         rot[:, N:N + (I + 1) * P], start=True, stop=True)
                    last.then_inc(S["s_done"], 1)
                if out:
                    wait(pe, S["acc_done"], n)
                    wait(pe, S["trc_done"], n + 1)
                    val = val_even[k % 2] if k < B else val_odd[k - B]
                    for I in range(TILES):
                        for J in range(I + 1):
                            last = pe.matmul(s.p7[:, I * P:(I + 1) * P],
                                             probT[:, OFF[I] + J * P:OFF[I] + (J + 1) * P],
                                             val[:, J * P:(J + 1) * P], start=(J == 0), stop=(J == I))
                    last.then_inc(S["av_done"], 1)
            steps(nc.tensor, a_step)

        @block.scalar
        def _(a):
            def build(part, i, off):
                h, par = i * 2 + off, off % 2
                if part == FRONT:
                    a.wait_ge(S["w_in"], h * 16 + 16)
                    wait(a, S["qk_done"], (h - 1) * B)
                    a.activation(wqk[par][0][:], wqk_raw[:], ACT.Copy).then_inc(S["w_hi"], 1)
                elif part == EXP:
                    a.wait_ge(S["arg_done"], h + 1)
                    a.activation(decay[par][:], decay[par][:], ACT.Exp).then_inc(S["decay_done"], 1)
                elif part == SQUARE:
                    a.wait_ge(S["decay_done"], h + 1)
                    wait(a, S["ek_done"], (h - 1) * B)
                    a.activation(decay2[par][:], decay[par][:], ACT.Square).then_inc(S["decay2_done"], 1)
                elif part == LN:
                    a.wait_ge(S["decay2_done"], h + 1)
                    a.activation(lam[par][:], decay2[par][:], ACT.Ln, bias=hp[par][:, A_PLUS_B:A_PLUS_B + 1],
                                 scale=hp[par][:, NEG_A:NEG_A + 1]).then_inc(S["lnv_done"], 1)

            def a_step(i, k, end):
                n = i * 16 + k
                out, score, proj = stages(k, end)
                m, c = n + 1, n + 2

                def square():
                    wait(a, S["swap_done"], c + 1)
                    wait(a, S["kn_done"], c)
                    a.activation(squares[:], swapped[:], ACT.Square).then_inc(S["sq_done"], 1)

                if out and k < B:
                    wait(a, S["v_done"], values_made(i, k))
                    for h, val in enumerate((val_even[k % 2], val_odd[k])):
                        last = a.activation(val[:].rearrange("p (j d) -> p j d", j=TILES),
                                            s.pV[:].rearrange("p (j h d) -> p h j d", j=TILES, h=2)[:, h], ACT.Copy)
                    last.then_inc(S["val_done"], 1)
                if proj:
                    wait(a, S["cos_done"], c + 1)
                    wait(a, S["sin_done"], c)
                    a.activation(swapped[0:DH, :], s.pQK[DH:P, :], ACT.Copy)
                    a.activation(swapped[DH:P, :], s.pQK[0:DH, :], ACT.Copy).then_inc(S["swap_done"], 1)
                    if not norms_late(k):
                        square()
                if out:
                    a.wait_ge(S["nmax_done"], n + 1)
                    for I in ORDER:
                        cols = slice(OFF[I], OFF[I] + (I + 1) * P)
                        last = a.activation(z[:, cols], z[:, cols], ACT.Exp, bias=nmax[:, I:I + 1],
                                            accum_out=rsum[:, k % 2, I:I + 1])
                    last.then_inc(S["exp_done"], 1)
                if proj and norms_late(k):
                    square()
                def copy_norms():
                    par = ((k + 2) // B) % 2
                    wait(a, S["kn_done"], c + 1)
                    wait(a, S["ek_done"], c)
                    a.activation(knorm[:], s.p6[:], ACT.Identity,
                                 bias=hp[par][:, NEG_NU_A:NEG_NU_A + 1]).then_inc(S["norm_done"], 1)

                if proj and not norms_late(k) and not norms_by_vector(k):
                    copy_norms()
                for part in (FRONT, EXP, SQUARE, LN):
                    if building(part, k, end):
                        build(part, i, building(part, k, end))
                if out:
                    a.wait_ge(S["tr_done"], n + 1)
                    wait(a, S["av_done"], n)
                    a.activation(probT[:], s.pS[:, 0:SW], ACT.Copy).then_inc(S["trc_done"], 1)
                if proj and norms_late(k):
                    copy_norms()
                if score:
                    wait(a, S["u_done"], m + 1)
                    a.activation(u[:], u[:], ACT.Ln).then_inc(S["ln_done"], 1)

            nc.scalar.preload_act_table_set("natural_log_exp_and_others")
            for part in (FRONT, EXP, SQUARE, LN):
                build(part, 0, 0)
            steps(nc.scalar, a_step)

        @block.gpsimd
        def _(g):
            def build(i, off):
                h, par = i * 2 + off, off % 2
                g.wait_ge(S["lnv_done"], h + 1)
                apart(g, S["pool_passed"])
                g.tensor_scalar(lam[par][:], lam[par][:], hp[par][:, LAM_SCALE:LAM_SCALE + 1],
                                hp[par][:, NEG_LN_NU:NEG_LN_NU + 1], ALU.mult, ALU.add).then_inc(S["lam0_done"], 1)

            def a_step(i, k, end):
                n = i * 16 + k
                out, score, proj = stages(k, end)
                if score:
                    m, par = n + 1, ((k + 1) // B) % 2
                    wait(g, S["decay2_done"], i * 2 + (k + 1) // B + 1)
                    wait(g, S["norm_done"], m + 1)
                    wait(g, S["sum_done"], m)
                    for I in ORDER:
                        cols = slice(OFF[I], OFF[I] + (I + 1) * P)
                        last = g.tensor_tensor(ek[:, cols], decay2[par][:, cols], knorm[:, 0:(I + 1) * P], ALU.mult)
                    last.then_inc(S["ek_done"], 1)
                if proj:
                    c, par = n + 2, ((k + 2) // B) % 2
                    wait(g, S["swap_done"], c + 1)
                    wait(g, S["s_done"], c)
                    wait(g, trig_in[par], i * 128 + ((k + 2) // (2 * B) + 1) * 128)
                    g.tensor_tensor(two(rot[:]), two(swapped[:]), both(sin[par]), ALU.mult).then_inc(S["sin_done"], 1)
                    wait(g, S["cos_done"], c + 1)
                    wait(g, S["sin_done"], c + 1)
                    g.tensor_tensor(rot[:], by_cos[:], rot[:], ALU.add).then_inc(S["rot_done"], 1)
                if building(LAM, k, end):
                    build(i, building(LAM, k, end))

            build(0, 0)
            steps(nc.gpsimd, a_step)

        @block.vector
        def _(v):
            def build_front(i, off):
                h, par = i * 2 + off, off % 2
                wait(v, S["norm_done"], (i * 2 + off - 1) * B)
                v.tensor_copy(hp[par][:], s.params[:, bass.ds(h, 1), :].rearrange("p a c -> p (a c)")).then_inc(S["hp_done"], 1)
                v.wait_ge(S["hp_done"], h + 1)
                v.tensor_scalar(decay[par][:], s.dist[:], hp[par][:, NEG_MU:NEG_MU + 1], MIN_EXP,
                                ALU.mult, ALU.max).then_inc(S["arg_done"], 1)

            def build_weights(i, off):
                h, par = i * 2 + off, off % 2
                v.wait_ge(S["w_hi"], h + 1)
                wait(v, S["qk_done"], (i * 2 + off - 1) * B)
                v.tensor_tensor(wqk[par][1][:], wqk_raw[:], wqk[par][0][:].bitcast(F32),
                                ALU.subtract).then_inc(S["w_lo"], 1)

            def build_back(i, off):
                h, par = i * 2 + off, off % 2
                v.wait_ge(S["lam0_done"], h + 1)
                for I in range(TILES):
                    cols = slice(OFF[I] + I * P, OFF[I] + (I + 1) * P)
                    last = v.scalar_tensor_tensor(lam[par][:, cols], s.upper[:], hp[par][:, INV_COEF:INV_COEF + 1],
                                                  lam[par][:, cols], ALU.mult, ALU.add)
                last.then_inc(S["lam_done"], 1)

            def accumulate(k, n):
                b = k % B
                v.wait_ge(S["av_done"], n + 1)
                v.wait_ge(S["rinv_done"], n + 1)
                for I in range(TILES):
                    xt = s.x_sb[:, b * TILES + I, :]
                    last = v.scalar_tensor_tensor(xt, s.p7[:, I * P:(I + 1) * P], rinv[:, k % 2, I:I + 1], xt,
                                                  ALU.mult, ALU.add)
                last.then_inc(S["acc_done"], 1)

            def a_step(i, k, end):
                k = k + 1
                n = i * 16 + k
                out, score, proj = stages(k, end)
                if proj:
                    c, par = n + 2, ((k + 2) // B) % 2
                    head = i * 2 + (k + 2) // B
                    wait(v, trig_in[par], i * 128 + ((k + 2) // (2 * B) + 1) * 128)
                    wait(v, S["qk_done"], c + 1)
                    wait(v, S["rot_done"], c)
                    v.tensor_tensor(two(by_cos[:]), two(s.pQK[:]), both(cos[par]), ALU.mult).then_inc(S["cos_done"], 1)
                if out:
                    par = (k // B) % 2
                    head = i * 2 + k // B
                    v.wait_ge(S["ln_done"], n + 1)
                    v.wait_ge(S["lam_done"], head + 1)
                    wait(v, S["exp_done"], n)
                    wait(v, S["tr_done"], n)
                    apart(v, S["dve_passed"])
                    for I in ORDER:
                        cols = slice(OFF[I], OFF[I] + (I + 1) * P)
                        last = v.tensor_tensor_reduce(z[:, cols], u[:, cols], lam[par][:, cols],
                                                      hp[par][:, COEF:COEF + 1], LOWEST, ALU.add, ALU.max,
                                                      zmax[:, I:I + 1])
                    last.then_inc(S["zred_done"], 1)
                    v.wait_ge(S["zred_done"], n + 1)
                    v.tensor_scalar(nmax[:], zmax[:], -1.0, None, ALU.mult).then_inc(S["nmax_done"], 1)
                if score:
                    m, par = n + 1, ((k + 1) // B) % 2
                    wait(v, S["decay_done"], i * 2 + (k + 1) // B + 1)
                    wait(v, S["s_done"], m + 1)
                    wait(v, S["zred_done"], m)
                    v.scalar_tensor_tensor(u[:], s.pS[:, 0:SW], -2.0, decay[par][:], ALU.mult,
                                           ALU.mult).then_inc(S["es_done"], 1)
                if score:
                    wait(v, S["ek_done"], m + 1)
                    wait(v, S["es_done"], m + 1)
                    wait(v, S["qn_done"], m + 1)
                    for I in ORDER:
                        cols = slice(OFF[I], OFF[I] + (I + 1) * P)
                        last = v.scalar_tensor_tensor(u[:, cols], ek[:, cols], qnorm[:, (k + 1) % 2, I:I + 1],
                                                      u[:, cols], ALU.add, ALU.add)
                    last.then_inc(S["sum_done"], 1)
                def query_norms():
                    wait(v, S["q2_done"], c + 1)
                    v.tensor_scalar(qnorm[:, k % 2, :], s.p5[:, 0:TILES], hp[((k + 2) // B) % 2][:, NU_AB:NU_AB + 1],
                                    None, ALU.add).then_inc(S["qn_done"], 1)

                if proj and not norms_late(k):
                    query_norms()
                if k >= 1:
                    accumulate(k - 1, n - 1)
                if proj and norms_late(k):
                    query_norms()
                if score:
                    wait(v, S["sum_done"], m + 1)
                    v.tensor_scalar(u[:], u[:], hp[par][:, U_MIN:U_MIN + 1], None, ALU.max).then_inc(S["u_done"], 1)
                if proj and norms_by_vector(k):
                    wait(v, S["kn_done"], c + 1)
                    wait(v, S["ek_done"], c)
                    v.tensor_scalar(knorm[:], s.p6[:], hp[((k + 2) // B) % 2][:, NEG_NU_A:NEG_NU_A + 1], None,
                                    ALU.add).then_inc(S["norm_done"], 1)
                if out:
                    v.wait_ge(S["exp_done"], n + 1)
                    v.reciprocal(rinv[:, k % 2, :], rsum[:, k % 2, :]).then_inc(S["rinv_done"], 1)
                if building(FRONT, k, end):
                    build_front(i, building(FRONT, k, end))
                if building(EXP, k, end):
                    build_weights(i, building(EXP, k, end))
                if building(MASK, k, end):
                    build_back(i, building(MASK, k, end))

            build_front(0, 0)
            build_weights(0, 0)
            build_back(0, 0)
            steps(nc.vector, a_step)
            v.wait_ge(S["acc_done"], PAIRS)
            for t in range(TT):
                last = v.bn_stats(stats[:, t, :], s.x_sb[:, t, :])
            last.then_inc(S["stat_done"], 1)
            v.wait_ge(S["stat_done"], 1)
            for t in range(TT):
                v.bn_aggr(s.mv[:, t, :], stats[:, t, :])


def program(nc, args, out):
    with ExitStack() as ctx:
        sb = lambda name, shape, dt=F32: ctx.enter_context(nc.sbuf_tensor(name, shape, dt))
        ps = lambda name, shape: ctx.enter_context(nc.psum_tensor(name, shape, F32))
        s = Shared(args, out)
        s.trig_d = nc.dram_tensor("trig_d", [3, H, DH // 2, N], F32, kind="Internal").ap()
        s.x_sb = sb("x_sb", [P, TT, D])
        s.xT = [sb(f"xT_{h}", [P, B * N], F32R) for h in ("hi", "lo")]
        s.mv = sb("mv", [P, TT, 2])
        s.w13 = [sb(f"w13_{h}", [P, 2 * HC * P], F32R) for h in ("hi", "lo")]
        s.w2s = [sb(f"w2_{h}", [P, HC * P], F32R) for h in ("hi", "lo")]
        s.wr = [sb(f"wr_{h}", [P, NE], F32R) for h in ("hi", "lo")]
        s.wp = [sb(f"wp_{h}", [P, H * P], F32R) for h in ("hi", "lo")]
        s.params = sb("params", [P, H, NPAR])
        s.ident = sb("ident", [P, P])
        s.ones = sb("ones", [P, P])
        s.dist = sb("dist", [P, SW])
        s.upper = sb("upper", [P, P])
        s.prio = sb("prio", [P, NE])
        s.pS = ps("pS", [P, 3 * N])
        s.pQK = ps("pQK", [P, 2 * N])
        s.pV = ps("pV", [P, 2 * N])
        s.p5, s.p6, s.p7 = s.pV[:, 0:N], s.pV[:, N:2 * N], ps("p7", [P, N])
        setup_phase(nc, s)
        for layer in range(2):
            with (nc.sbuf_tensor(f"wT{layer}", [2 * NE, B * N], F32R) as wT,
                  nc.sbuf_tensor(f"selr{layer}", [2 * NE, HC * P], F32R) as selr):
                s.wT, s.selr = wT, selr
                norm_phase(nc, s, f"n{layer}", True)
                ffn_phase(nc, s, f"f{layer}", layer == 1, layer == 0)
            if layer == 0:
                norm_phase(nc, s, "na", False)
                attention_phase(nc, s)


def kernel(**inputs):
    import concourse.bacc as bacc
    from concourse.bass_utils import run_bass_kernel_spmd

    a = {k[3:]: np.asarray(v) for k, v in inputs.items()}
    c = np.ascontiguousarray

    def heads(w):
        return w.reshape(D, 2, H, DH).transpose(2, 0, 1, 3).reshape(H, D, 2 * DH)

    row, col = np.arange(P)[:, None], np.arange(N)[None, :]
    dist = np.zeros((P, SW), np.float32)
    for tile, off in OFF.items():
        w = (tile + 1) * P
        dist[:, off:off + w] = np.abs(tile * P + row - col[:, :w])
    unit = np.arange(NE * FH)[None, :] // FH
    arrays = {
        "x": c(a["attn_x"]),
        "wqk": c(np.concatenate([heads(a["attn_Wq"]), heads(a["attn_Wk"])], axis=2)),
        "wv": c(heads(a["attn_Wv"])),
        "wo": c(a["attn_Wo"].reshape(2, H, DH, D).transpose(1, 0, 2, 3).reshape(H, 2 * DH, D)),
        "omega": c(a["attn_omega"].reshape(4, P).T),
        "head_vec": c(np.stack([a["attn_" + n] for n in (
            "mu_raw", "sigma_raw", "eta_raw", "gamma_raw", "nu_raw", "tau")])),
        "w_router": c(a["ffn_w_router"].T),
        "w1": c(a["ffn_w1"]), "w3": c(a["ffn_w3"]), "w2": c(a["ffn_w2"].reshape(NE * FH, D)),
        "t_row": np.arange(N, dtype=np.float32),
        "ident_d": np.eye(P, dtype=np.float32),
        "dist_d": dist,
        "upper_d": np.where(np.arange(P)[None, :] > row, MASKED, 0.0).astype(np.float32),
        "prio_d": NE - np.arange(NE, dtype=np.float32),
        "sel": c((unit == np.arange(2 * NE)[:, None] % NE).astype(np.float32)),
    }
    nc = bacc.Bacc("TRN2", target_bir_lowering=False, num_devices=1)
    args = {n: nc.dram_tensor(f"in_{n}", v.shape, F32, kind="ExternalInput").ap() for n, v in arrays.items()}
    out = nc.dram_tensor("out_x", (B, N, D), F32, kind="ExternalOutput").ap()
    program(nc, args, out)
    r = run_bass_kernel_spmd(nc, [{f"in_{n}": v for n, v in arrays.items()}], core_ids=[0])
    return r.results[0]["out_x"]
```
